# Optimizing a Trainium2 kernel written in Bass

```python
import numpy as np
import jax
import jax.numpy as jnp

def _softmax(x, axis=-1):
    return jax.nn.softmax(x, axis=axis)

def _gelu(x):
    return jax.nn.gelu(x, approximate=True)

def _silu(x):
    return jax.nn.silu(x)

def _sigmoid(x):
    return jax.nn.sigmoid(x)

def _layernorm(x, axis=-1, eps=1e-05):
    m = jnp.mean(x, axis=axis, keepdims=True)
    v = jnp.var(x, axis=axis, keepdims=True)
    return (x - m) / jnp.sqrt(v + eps)

def _scatter_add(tgt, idx, src, axis=0):
    return tgt.at[idx].add(src)

def _segment_sum(src, seg, n):
    return jax.ops.segment_sum(src, seg, n)
kernel_name = 'mk_xattn_seq_d1_seqx_r4_7878ed'

def setup_inputs(seed: int=0):
    np.random.seed(seed)
    _w = jnp.asarray

    def _rec_inputs():
        import jax
        import jax.numpy as jnp
        _rk = jax.random.key(seed)
        x = -0.0003929 + 0.9999 * jax.random.normal(jax.random.fold_in(_rk, 1), (16, 100, 512), jnp.float32)
        _lenS = 100 - jax.random.randint(jax.random.fold_in(_rk, 7), (16,), 0, max(1, 100 // 4) + 1, jnp.int32)
        _lenS2 = 361 - jax.random.randint(jax.random.fold_in(_rk, 8), (16,), 0, max(1, 361 // 4) + 1, jnp.int32)
        _ctx_2048P = jax.random.normal(jax.random.fold_in(_rk, 11), (16, 16, 512), jnp.float32)
        _ctx_2048c = jax.random.dirichlet(jax.random.fold_in(_rk, 511), 0.3 * jnp.ones((16,), jnp.float32), (16, 361))
        _ctx_2048t = jnp.einsum('bsk,bkd->bsd', _ctx_2048c, _ctx_2048P)
        _ctx_2048t = _ctx_2048t * jax.lax.rsqrt(jnp.mean(jnp.square(_ctx_2048t)) + 1e-12) * 0.953939
        ctx_2048 = -8.57375e-05 + 0.999917 * (_ctx_2048t + 0.3 * jax.random.normal(jax.random.fold_in(_rk, 611), (16, 361, 512), jnp.float32))
        _validS = jnp.arange(100)[None, :] < _lenS[:, None]
        _validS2 = jnp.arange(361)[None, :] < _lenS2[:, None]
        _causal = jnp.tril(jnp.ones((100, 100), dtype=bool))
        mask_BxS2_bf1 = jnp.ones((16, 361), dtype=bool)
        return (x, ctx_2048, mask_BxS2_bf1)
    x, ctx_2048, mask_BxS2_bf1 = _rec_inputs()

    def _L0_xattn_setup():
        import jax, jax.numpy as jnp
        import numpy as np
        HIDDEN = 512
        HEADS = 16
        HEAD_DIM = HIDDEN // HEADS
        LN_EPS = 1e-05
        GATE_INIT = 0.5

        def _layer_norm(x, gamma, beta):
            mu = jnp.mean(x, axis=-1, keepdims=True)
            var = jnp.mean(jnp.square(x - mu), axis=-1, keepdims=True)
            return (x - mu) * jax.lax.rsqrt(var + LN_EPS) * gamma + beta
        key = jax.random.key(seed)
        ks = jax.random.split(key, 8)
        B, T_TEXT, T_AUDIO = (4, 512, 375)
        s = 0.02
        return {'hidden_states': jax.random.normal(ks[0], (B, T_TEXT, HIDDEN), jnp.float32), 'audio_kv': jax.random.normal(ks[1], (B, T_AUDIO, HIDDEN), jnp.float32), 'audio_attention_mask': jnp.ones((B, T_AUDIO), dtype=bool), 'Wq': jax.random.normal(ks[2], (HIDDEN, HIDDEN), jnp.float32) * s, 'Wk': jax.random.normal(ks[3], (HIDDEN, HIDDEN), jnp.float32) * s, 'Wv': jax.random.normal(ks[4], (HIDDEN, HIDDEN), jnp.float32) * s, 'Wo': jax.random.normal(ks[5], (HIDDEN, HIDDEN), jnp.float32) * s, 'ln_gamma': jnp.ones((HIDDEN,), jnp.float32), 'ln_beta': jnp.zeros((HIDDEN,), jnp.float32), 'gate': jnp.array([GATE_INIT], jnp.float32)}
    _L0_xattn_all = _L0_xattn_setup()
    _L0_xattn_in = {k: v for k, v in _L0_xattn_all.items() if k in ('Wq', 'Wk', 'Wv', 'Wo', 'ln_gamma', 'ln_beta', 'gate')}
    del _L0_xattn_all
    return {'x': x, 'ctx_2048': ctx_2048, 'mask_BxS2_bf1': mask_BxS2_bf1, 'L0_xattn_Wq': _L0_xattn_in['Wq'], 'L0_xattn_Wk': _L0_xattn_in['Wk'], 'L0_xattn_Wv': _L0_xattn_in['Wv'], 'L0_xattn_Wo': _L0_xattn_in['Wo'], 'L0_xattn_ln_gamma': _L0_xattn_in['ln_gamma'], 'L0_xattn_ln_beta': _L0_xattn_in['ln_beta'], 'L0_xattn_gate': _L0_xattn_in['gate']}

def reference(x, ctx_2048, mask_BxS2_bf1, L0_xattn_Wq, L0_xattn_Wk, L0_xattn_Wv, L0_xattn_Wo, L0_xattn_ln_gamma, L0_xattn_ln_beta, L0_xattn_gate):
    import jax
    import jax.numpy as jnp

    def _L0_xattn_ref(hidden_states, audio_kv, audio_attention_mask, Wq, Wk, Wv, Wo, ln_gamma, ln_beta, gate):
        import jax, jax.numpy as jnp
        import numpy as np
        HIDDEN = 512
        HEADS = 16
        HEAD_DIM = HIDDEN // HEADS
        LN_EPS = 1e-05
        GATE_INIT = 0.5

        def _layer_norm(x, gamma, beta):
            mu = jnp.mean(x, axis=-1, keepdims=True)
            var = jnp.mean(jnp.square(x - mu), axis=-1, keepdims=True)
            return (x - mu) * jax.lax.rsqrt(var + LN_EPS) * gamma + beta
        B, Tt, D = hidden_states.shape
        Ta = audio_kv.shape[1]
        scale = HEAD_DIM ** (-0.5)
        a = _layer_norm(audio_kv, ln_gamma, ln_beta)
        Q = (hidden_states @ Wq.T).reshape(B, Tt, HEADS, HEAD_DIM).transpose(0, 2, 1, 3)
        K = (a @ Wk.T).reshape(B, Ta, HEADS, HEAD_DIM).transpose(0, 2, 1, 3)
        V = (a @ Wv.T).reshape(B, Ta, HEADS, HEAD_DIM).transpose(0, 2, 1, 3)
        scores = jnp.einsum('bhtd,bhsd->bhts', Q, K) * scale
        mask = audio_attention_mask[:, None, None, :]
        scores = jnp.where(mask, scores, jnp.float32(-jnp.inf))
        attn = jax.nn.softmax(scores, axis=-1)
        out = jnp.einsum('bhts,bhsd->bhtd', attn, V)
        out = out.transpose(0, 2, 1, 3).reshape(B, Tt, D)
        out = out @ Wo.T
        return hidden_states + jnp.tanh(gate) * out
    x = _L0_xattn_ref(x, ctx_2048, mask_BxS2_bf1, L0_xattn_Wq, L0_xattn_Wk, L0_xattn_Wv, L0_xattn_Wo, L0_xattn_ln_gamma, L0_xattn_ln_beta, L0_xattn_gate)
    return x

_drawn_inputs = setup_inputs


def setup_inputs(seed=0):
    import zlib

    import numpy as np

    out = dict(_drawn_inputs(seed))
    spreads = {'L0_xattn_ln_gamma': (1.0, 0.6), 'L0_xattn_ln_beta': (0.0, 0.8)}
    factors = {'L0_xattn_Wq': 8.0, 'L0_xattn_Wk': 8.0}
    for name, (base, spread) in spreads.items():
        noise = np.random.default_rng([zlib.crc32(name.encode()), seed]).standard_normal(out[name].shape)
        drawn = base * np.exp(spread * noise) if base else spread * noise
        out[name] = jnp.asarray(drawn.astype(out[name].dtype))
    for name, factor in factors.items():
        out[name] = (out[name] * factor).astype(out[name].dtype)
    return out
```

```python
from contextlib import ExitStack

import concourse.bass as bass
from concourse import mybir

F32 = mybir.dt.float32
F32R = mybir.dt.float32r
I32 = mybir.dt.int32
ALU = mybir.AluOpType
ACT = mybir.ActivationFunctionType

P = 128
HEAD_DIM = 32
LN_EPS = 1e-5
MASKED = -1e30
RSQRT_MAGIC = float(0x5F3759DF)
NEWTON_STEPS = 3
LN_STEPS = 5 + 3 * NEWTON_STEPS


class Batch:

    def __init__(self, n, parity, pair):
        self.n, self.parity, self.pair = n, parity, pair

    def after(self, k):
        p = self.parity + k
        return Batch(self.n + k, p % 2, self.pair + p // 2)


def batch(n):
    return Batch(n, n % 2, n // 2)


def xattn_program(nc, x, xT, ctx, mask, wqT, wkT, wvT, woT, gamma, beta, gate, out):
    B, T, D = x.shape
    S = ctx.shape[1]
    H = D // HEAD_DIM
    DC = D // P
    HG = P // HEAD_DIM
    G = H // HG
    SC = (S + P - 1) // P
    S_LAST = S - (SC - 1) * P
    S_EVEN = S + S % 2
    GT = HG * T
    QB = 4
    QN = B // QB
    QCOLS = QB * T
    VW = HEAD_DIM + 2
    OV = HEAD_DIM + 1
    U_NT, U_K, U_OUT, U_V = 0, DC, 2 * DC, 2 * DC + 1
    UNITS = 2 * DC + SC
    assert D == 512 and G == DC and SC == 3 and QCOLS <= 400 and GT <= 512 and B % QB == 0
    rows = [P] * (SC - 1) + [S_LAST]
    scale = HEAD_DIM ** -0.5

    sums_dram = nc.dram_tensor("sums_scratch", [2, H, T], F32, kind="Internal").ap()
    recip_dram = nc.dram_tensor("recip_scratch", [2, H, T], F32, kind="Internal").ap()

    with ExitStack() as stack:
        def sb(name, shape, dt=F32):
            return stack.enter_context(nc.sbuf_tensor(name, shape, dt))

        def sem(name):
            return stack.enter_context(nc.semaphore(name))

        ctx_sb = sb("ctx_sb", [P, 2, SC, D])
        nTh = sb("nTh", [P, DC, QCOLS], F32R)
        nTl = sb("nTl", [P, DC, QCOLS], F32R)
        wqh = sb("wqh", [P, DC, D], F32R)
        wql = sb("wql", [P, DC, D], F32R)
        wkh = sb("wkh", [P, DC, D], F32R)
        wkl = sb("wkl", [P, DC, D], F32R)
        wvh = sb("wvh", [P, DC, D], F32R)
        wvl = sb("wvl", [P, DC, D], F32R)
        wo_sb = sb("wo_sb", [P, DC, D])
        q_sb = sb("q_sb", [P, G, B * T])
        kTh = sb("kTh", [P, 2, G, SC * P], F32R)
        kTl = sb("kTl", [P, 2, G, SC * P], F32R)
        v_sb = sb("v_sb", [P, 2, SC, H, VW])
        qblk_even = sb("qblk_even", [P, 2, G, HG, T], F32R)
        probs = sb("probs", [P, G, SC, GT])
        colmax = sb("colmax", [P, 2, GT])
        rowmax = sb("rowmax", [P, 2, GT])
        attn_raw = sb("attn_raw", [P, 2, G * T])
        recip_bc = sb("recip_bc", [P, 2, G * T])
        attnT = sb("attnT", [P, G, T])
        sums = sb("sums", [H, T])
        recips = sb("recips", [H, T])
        io = sb("io", [P, 2, 2, D])
        x_rows, out_rows = io[:, 0], io[:, 1]
        ident = sb("ident", [P, P])
        mask_u8 = sb("mask_u8", [B, S], mybir.dt.uint8)
        mask_f = sb("mask_f", [B, SC * P])
        mask_bias = sb("mask_bias", [P, B * SC])
        maskT = sb("maskT", [P, SC * B])
        ones = sb("ones", [P, P])
        key_count = sb("key_count", [P, B])
        mask_now = sb("mask_now", [P, 2, SC])
        gamma_sb = sb("gamma_sb", [P, DC])
        beta_sb = sb("beta_sb", [P, DC])
        beta_bc = sb("beta_bc", [P, DC, P])
        k_bias = sb("k_bias", [P, G])
        v_bias = sb("v_bias", [P, D])
        gate_sb = sb("gate_sb", [P, 2])
        stats = sb("stats", [P, SC, 6])
        mean_var = sb("mean_var", [P, SC, 2])
        var_eps = sb("var_eps", [P, SC])
        half_bits = sb("half_bits", [P, SC], I32)
        rstd = sb("rstd", [P, SC])
        newton_a = sb("newton_a", [P, SC])
        newton_b = sb("newton_b", [P, SC])

        qblk_odd_h = wqh[:].rearrange("p a b -> p (a b)")[:, 0:G * GT].rearrange(
            "p (g j t) -> p g j t", g=G, j=HG)
        qblk_odd_l = wql[:].rearrange("p a b -> p (a b)")[:, 0:G * GT].rearrange(
            "p (g j t) -> p g j t", g=G, j=HG)
        qblk_h = [qblk_even[:, 0], qblk_odd_h]
        qblk_l = [qblk_even[:, 1], qblk_odd_l]
        wq_raw = probs[:].rearrange("p a c n -> p (a c n)")[:, 0:DC * D].rearrange("p (k n) -> p k n", k=DC)
        wv_raw = wq_raw
        wk_raw = io[:].rearrange("p a b n -> p (a b) n")
        v_flat = v_sb[:].rearrange("p a c h w -> p (a c h w)")
        xT_raw = [v_flat[:, i * DC * QCOLS:(i + 1) * DC * QCOLS].rearrange("p (k n) -> p k n", k=DC)
                  for i in range(2)]

        ps_s = stack.enter_context(nc.psum_tensor("ps_s", [P, SC, 512], F32))
        ps_av = stack.enter_context(nc.psum_tensor("ps_av", [P, 2, 512], F32))
        ps_w = stack.enter_context(nc.psum_tensor("ps_w", [P, 3, 512], F32))
        mask_bank = ps_av[:, 1]
        q_banks = [[ps_s[:, 0], ps_s[:, 1], ps_s[:, 2], ps_w[:, 0]],
                   [ps_w[:, 1], ps_w[:, 2], ps_av[:, 0], ps_av[:, 1]]]

        small_in = sem("small_in")
        mask_in = sem("mask_in")
        wq_in = [sem(f"wq_in{k}") for k in range(DC)]
        wk_in, wv_in, wo_in = sem("wk_in"), sem("wv_in"), sem("wo_in")
        xT_first = [sem(f"xT_first{k}") for k in range(DC)]
        xT_in = [sem("xT_in0"), sem("xT_in1")]
        ctx_in = [sem("ctx_in0"), sem("ctx_in1")]
        x_in = [sem("x_in0"), sem("x_in1")]
        ident_ready = sem("ident_ready")
        setup = sem("setup")
        mask_cast = sem("mask_cast")
        maskT_in_psum, mask_bias_ready = sem("maskT_in_psum"), sem("mask_bias_ready")
        maskT_kept, count_in_psum = sem("maskT_kept"), sem("count_in_psum")
        gate_ready = sem("gate_ready")
        wq_hi, wq_lo = sem("wq_hi"), sem("wq_lo")
        wk_hi, wk_lo = sem("wk_hi"), sem("wk_lo")
        wv_hi, wv_lo = sem("wv_hi"), sem("wv_lo")
        xT_hi, xT_lo = sem("xT_hi"), sem("xT_lo")
        xT_used = sem("xT_used")
        q_in_psum, q_kept = sem("q_in_psum"), sem("q_kept")
        kb_in_psum, kb_ready = sem("kb_in_psum"), sem("kb_ready")
        vb_in_psum, vb_ready = sem("vb_in_psum"), sem("vb_ready")
        beta_bc_ready = sem("beta_bc_ready")
        qblk_zeroed = sem("qblk_zeroed")
        pads_ready = sem("pads_ready")
        mask_copied = sem("mask_copied")
        waited_dve, waited_pool = sem("waited_dve"), sem("waited_pool")
        ln_step = sem("ln_step")
        normed = sem("normed")
        nT_in_psum, k_in_psum, v_in_psum = sem("nT_in_psum"), sem("k_in_psum"), sem("v_in_psum")
        out_in_psum = sem("out_in_psum")
        nT_hi, k_hi = sem("nT_hi"), sem("k_hi")
        drained = sem("drained")
        qblk_hi, qblk_ready = sem("qblk_hi"), sem("qblk_ready")
        s_in_psum, s_kept = sem("s_in_psum"), sem("s_kept")
        max_partial, colmax_ready, rowmax_ready = sem("max_partial"), sem("colmax_ready"), sem("rowmax_ready")
        shifted, probs_ready, av_done = sem("shifted"), sem("probs_ready"), sem("av_done")
        attn_kept = sem("attn_kept")
        sums_out, sums_in = sem("sums_out"), sem("sums_in")
        recips_ready, recips_out, recips_in = sem("recips_ready"), sem("recips_out"), sem("recips_in")
        attnT_ready = sem("attnT_ready")
        out_ready = sem("out_ready")
        stored = sem("stored")

        block = stack.enter_context(nc.Block())

        def steps(engine, step):
            step(batch(0), True, True, False)
            step(batch(1), True, True, True)
            with engine.Fori(1, B // 2 - 1) as i:
                step(Batch(2 * i, 0, i), True, True, True)
                step(Batch(2 * i + 1, 1, i), True, True, True)
            step(batch(B - 2), True, False, True)
            step(batch(B - 1), False, False, True)

        @block.sync
        def _(sp):
            def load_ctx(b, again):
                if again:
                    sp.wait_ge(nT_in_psum, DC * (b.n - 1))
                sp.dma_start(ctx_sb[:, b.parity, 0:SC - 1],
                             ctx[b.n, 0:(SC - 1) * P].rearrange("(c p) d -> p c d", p=P)
                             ).then_inc(ctx_in[b.parity], 16)
                sp.dma_start(ctx_sb[0:S_LAST, b.parity, SC - 1],
                             ctx[b.n, (SC - 1) * P:S]).then_inc(ctx_in[b.parity], 16)

            def load_xT(i, again):
                if again:
                    sp.wait_ge(xT_lo, DC * (i - 1))
                sp.dma_start(xT_raw[i % 2], xT[:, i * QCOLS:(i + 1) * QCOLS].rearrange(
                    "(k p) n -> p k n", p=P)).then_inc(xT_in[i % 2], 16)

            def weights(w):
                return w.rearrange("(k p) n -> p k n", p=P)

            for k in range(DC):
                sp.dma_start(wq_raw[:, k], wqT[k * P:(k + 1) * P]).then_inc(wq_in[k], 16)
                sp.dma_start(xT_raw[0][:, k], xT[k * P:(k + 1) * P, 0:QCOLS]).then_inc(xT_first[k], 16)
                if k == 0:
                    sp.dma_start(mask_u8[:], mask).then_inc(mask_in, 16)
            load_xT(1, False)
            sp.dma_start(gamma_sb[:], gamma).then_inc(small_in, 16)
            sp.dma_start(beta_sb[:], beta).then_inc(small_in, 16)
            sp.dma_start(gate_sb[:, 0:1], gate[None, :].to_broadcast([P, 1])).then_inc(small_in, 16)
            load_ctx(batch(0), False)
            sp.dma_start(wk_raw, weights(wkT)).then_inc(wk_in, 16)
            load_ctx(batch(1), False)
            sp.wait_ge(wq_lo, DC)
            sp.dma_start(wv_raw, weights(wvT)).then_inc(wv_in, 16)
            sp.dma_start(wo_sb[:], weights(woT)).then_inc(wo_in, 16)
            for i in range(2, QN):
                load_xT(i, True)
            def load_x(b, again):
                if again:
                    sp.wait_ge(out_ready, b.n - 1)
                sp.dma_start(x_rows[0:T, b.parity], x[b.n]).then_inc(x_in[b.parity], 16)

            sp.wait_ge(wk_lo, DC)
            sp.wait_ge(kb_in_psum, 1)
            load_x(batch(0), False)
            load_x(batch(1), False)

            def sums_round_trip(b):
                sp.wait_ge(attn_kept, 2 * b.n + 2)
                flat = sums_dram[b.parity].rearrange("(a s g) t -> a s (g t)", a=2, s=2)
                for half in range(2):
                    row = 64 * half + HEAD_DIM
                    sp.dma_start(flat[half:half + 1], attn_raw[row:row + 1]).then_inc(sums_out, 16)
                sp.wait_ge(sums_out, 32 * b.n + 32)
                sp.dma_start(sums[:], sums_dram[b.parity]).then_inc(sums_in, 16)
                sp.wait_ge(recips_ready, b.n + 1)
                sp.dma_start(recip_dram[b.parity], recips[:]).then_inc(recips_out, 16)
                sp.wait_ge(recips_out, 16 * b.n + 16)
                back = recip_dram[b.parity].rearrange("(a s g) t -> a (s g t)", a=2, s=2)
                for half in range(2):
                    lo = 64 * half
                    sp.dma_start(recip_bc[lo:lo + HEAD_DIM].rearrange("p a n -> p (a n)"),
                                 back[half:half + 1].to_broadcast([HEAD_DIM, 2 * G * T])
                                 ).then_inc(recips_in, 16)

            def store(b):
                sp.wait_ge(out_ready, b.n + 1)
                sp.dma_start(out[b.n], out_rows[0:T, b.parity]).then_inc(stored, 16)

            def step(b, more, more2, prev):
                if more2:
                    load_ctx(b.after(2), True)
                if prev:
                    sums_round_trip(b.after(-1))
                    store(b.after(-1))
                    if more:
                        load_x(b.after(1), True)

            steps(sp, step)
            last = batch(B - 1)
            sums_round_trip(last)
            store(last)
            sp.wait_ge(stored, 16 * B)

        @block.tensor
        def _(pe):
            def split_product(dst, wh, wl, mh, ml, start, stop):
                nc.tensor.matmul(dst, wh, mh, start=start, stop=False)
                nc.tensor.matmul(dst, wh, ml, start=False, stop=False)
                return nc.tensor.matmul(dst, wl, mh, start=False, stop=stop)

            pe.wait_ge(ident_ready, 2)
            pe.wait_ge(mask_cast, 1)
            for c in range(SC):
                last = nc.tensor.transpose(mask_bank[:, c * B:(c + 1) * B], mask_f[:, c * P:(c + 1) * P],
                                           ident[0:B, 0:B])
            last.then_inc(maskT_in_psum, 1)
            pe.wait_ge(maskT_kept, 1)
            nc.tensor.matmul(mask_bank[:, SC * B:2 * SC * B], ones[:], maskT[:], start=True,
                             stop=True).then_inc(count_in_psum, 1)

            for i in range(QN):
                for k in range(DC):
                    if i == 0:
                        pe.wait_ge(wq_lo, k + 1)
                    pe.wait_ge(xT_lo, DC * i + k + 1)
                    for g in range(G):
                        if k == 0 and i == 1 and g == G - 1:
                            pe.wait_ge(mask_bias_ready, 1)
                        if k == 0 and i >= 2:
                            pe.wait_ge(q_kept, G * (i - 2) + g + 1)
                        last = split_product(q_banks[i % 2][g][:, 0:QCOLS],
                                             wqh[:, k, g * P:(g + 1) * P], wql[:, k, g * P:(g + 1) * P],
                                             nTh[:, k], nTl[:, k], k == 0, k == DC - 1)
                        if k == DC - 1 and g < G - 1:
                            last.then_inc(q_in_psum, 1)
                    last.then_inc(xT_used, 1)

            def bank_free(b, u):
                if not (isinstance(b.n, int) and UNITS * b.n + u - 2 <= 0):
                    pe.wait_ge(drained, UNITS * b.n + u - 2)

            def transposes(b, first, last_chunk):
                pe.wait_ge(normed, b.n + 1)
                for k in range(first, last_chunk + 1):
                    u = U_NT + k
                    bank_free(b, u)
                    for c in range(SC):
                        last = nc.tensor.transpose(ps_w[:, u % 3, c * P:c * P + rows[c]],
                                                   ctx_sb[0:rows[c], b.parity, c, k * P:(k + 1) * P],
                                                   ident[0:rows[c], 0:rows[c]])
                    last.then_inc(nT_in_psum, 1)

            def k_projection(b, g):
                u = U_K + g
                if g:
                    pe.wait_ge(drained, UNITS * b.n + max(DC, u - 2))
                for k in range(DC):
                    if g == 0:
                        pe.wait_ge(drained, UNITS * b.n + max(k + 1, u - 2))
                    last = split_product(ps_w[:, u % 3, 0:S_EVEN],
                                         wkh[:, k, g * P:(g + 1) * P], wkl[:, k, g * P:(g + 1) * P],
                                         nTh[:, k, 0:S_EVEN], nTl[:, k, 0:S_EVEN], k == 0, k == DC - 1)
                last.then_inc(k_in_psum, 1)

            def v_projection(b, c):
                u = U_V + c
                if c < SC - 1:
                    pe.wait_ge(drained, UNITS * b.n + U_K + 3 + c)
                elif not (isinstance(b.n, int) and b.n < 2):
                    pe.wait_ge(out_ready, b.n - 1)
                for k in range(DC):
                    at = slice(c * P, c * P + rows[c])
                    last = split_product(ps_w[0:rows[c], u % 3, :], nTh[:, k, at], nTl[:, k, at],
                                         wvh[:, k], wvl[:, k], k == 0, k == DC - 1)
                last.then_inc(v_in_psum, 1)

            def scores(b, g):
                if g == 0:
                    pe.wait_ge(drained, UNITS * b.n + U_K + G)
                    pe.wait_ge(qblk_ready, b.n + 1)
                for c in range(SC):
                    if not (isinstance(b.n, int) and b.n == 0 and g == 0):
                        pe.wait_ge(s_kept, SC * (G * b.n + g - 1) + c + 1)
                    at = slice(c * P, (c + 1) * P)
                    split_product(ps_s[:, c, 0:GT], kTh[:, b.parity, g, at], kTl[:, b.parity, g, at],
                                  qblk_h[b.parity][:, g], qblk_l[b.parity][:, g], True, True
                                  ).then_inc(s_in_psum, 1)

            def weighted_values(b, g):
                pe.wait_ge(probs_ready, G * b.n + g + 1)
                if g == 0:
                    pe.wait_ge(drained, UNITS * b.n + UNITS)
                    if not (isinstance(b.n, int) and b.n == 0):
                        pe.wait_ge(attn_kept, 2 * b.n)
                for slot in range(2):
                    for c in range(SC):
                        for half in range(2):
                            j = 2 * slot + half
                            last = nc.tensor.matmul(
                                ps_av[64 * half:64 * half + OV, slot, g * T:(g + 1) * T],
                                v_sb[0:rows[c], b.parity, c, HG * g + j, 0:OV],
                                probs[0:rows[c], g, c, j * T:(j + 1) * T],
                                start=c == 0, stop=c == SC - 1)
                last.then_inc(av_done, 1)

            def out_projection(b):
                pe.wait_ge(attnT_ready, b.n + 1)
                for g in range(G):
                    last = nc.tensor.matmul(ps_w[0:T, U_OUT % 3, :], attnT[:, g], wo_sb[:, g],
                                            start=g == 0, stop=g == G - 1)
                last.then_inc(out_in_psum, 1)

            pe.wait_ge(q_kept, G * (QN - 1))
            pe.wait_ge(wk_in, 16)
            pe.wait_ge(small_in, 48)
            for g in range(G):
                for k in range(DC):
                    last = nc.tensor.matmul(ps_s[:, 1, g:g + 1], wk_raw[:, k, g * P:(g + 1) * P],
                                            beta_sb[:, k:k + 1], start=k == 0, stop=k == DC - 1)
            last.then_inc(kb_in_psum, 1)
            pe.wait_ge(q_kept, G * QN)
            transposes(batch(0), 0, DC - 1)
            pe.wait_ge(wv_in, 16)
            pe.wait_ge(beta_bc_ready, 1)
            for k in range(DC):
                last = nc.tensor.matmul(ps_s[:, 2, :], beta_bc[:, k], wv_raw[:, k], start=k == 0,
                                        stop=k == DC - 1)
            last.then_inc(vb_in_psum, 1)
            pe.wait_ge(wk_lo, DC)
            for g in range(G):
                k_projection(batch(0), g)
            pe.wait_ge(wv_lo, DC)
            for c in range(SC):
                v_projection(batch(0), c)

            def step(b, more, more2, prev):
                n = b.after(1)
                if more:
                    transposes(n, 0, DC - 2)
                scores(b, 0)
                if more:
                    transposes(n, DC - 1, DC - 1)
                    k_projection(n, 0)
                scores(b, 1)
                if more:
                    k_projection(n, 1)
                scores(b, 2)
                if more:
                    k_projection(n, 2)
                weighted_values(b, 0)
                if more:
                    k_projection(n, 3)
                scores(b, 3)
                weighted_values(b, 1)
                if prev:
                    pe.wait_ge(drained, UNITS * n.n + (U_K + 2 if more else 0))
                    out_projection(b.after(-1))
                if more:
                    v_projection(n, 0)
                weighted_values(b, 2)
                if more:
                    v_projection(n, 1)
                weighted_values(b, 3)
                if more:
                    v_projection(n, 2)

            pe.wait_ge(vb_ready, 1)
            pe.wait_ge(kb_ready, 1)
            pe.wait_ge(wo_in, 16)
            steps(pe, step)
            pe.wait_ge(out_ready, B - 1)
            out_projection(batch(B - 1))

        @block.scalar
        def _(act):
            def split_xT(i):
                for k in range(DC):
                    if i == 0:
                        act.wait_ge(wq_in[k], 16)
                        nc.scalar.copy(wqh[:, k], wq_raw[:, k]).then_inc(wq_hi, 1)
                        act.wait_ge(xT_first[k], 16)
                    elif k == 0:
                        act.wait_ge(xT_in[i % 2], 16 * ((i + 1) // 2))
                    if i >= 1:
                        act.wait_ge(xT_used, DC * (i - 1) + k + 1)
                    nc.scalar.copy(nTh[:, k], xT_raw[i % 2][:, k]).then_inc(xT_hi, 1)

            def keep_q(i):
                for g in range(G):
                    if g < G - 1:
                        act.wait_ge(q_in_psum, (G - 1) * i + g + 1)
                    else:
                        act.wait_ge(xT_used, DC * (i + 1))
                    nc.scalar.copy(q_sb[:, g, i * QCOLS:(i + 1) * QCOLS],
                                   q_banks[i % 2][g][:, 0:QCOLS]).then_inc(q_kept, 1)

            split_xT(0)
            act.wait_ge(small_in, 48)
            nc.scalar.activation(gate_sb[:, 1:2], gate_sb[:, 0:1], ACT.Tanh).then_inc(gate_ready, 1)
            split_xT(1)
            act.wait_ge(wk_in, 16)
            for k in range(DC):
                nc.scalar.activation(wkh[:, k], wk_raw[:, k], ACT.Identity,
                                     scale=gamma_sb[:, k:k + 1]).then_inc(wk_hi, 1)
            keep_q(0)
            split_xT(2)
            act.wait_ge(wv_in, 16)
            for k in range(DC):
                nc.scalar.activation(wvh[:, k], wv_raw[:, k], ACT.Identity,
                                     scale=gamma_sb[:, k:k + 1]).then_inc(wv_hi, 1)
            keep_q(1)
            split_xT(3)
            keep_q(2)
            keep_q(3)

            def keep_nT_hi(b, first, last_chunk):
                for k in range(first, last_chunk + 1):
                    act.wait_ge(nT_in_psum, DC * b.n + k + 1)
                    nc.scalar.copy(nTh[:, k, 0:S], ps_w[:, (U_NT + k) % 3, 0:S]).then_inc(nT_hi, 1)

            def keep_k_hi(b, g):
                act.wait_ge(k_in_psum, G * b.n + g + 1)
                nc.scalar.activation(kTh[:, b.parity, g, 0:S], ps_w[:, (U_K + g) % 3, 0:S],
                                     ACT.Identity, bias=k_bias[:, g:g + 1]).then_inc(k_hi, 1)

            def block_q_hi(b):
                for j in range(HG):
                    at = slice(HEAD_DIM * j, HEAD_DIM * (j + 1))
                    nc.scalar.copy(qblk_h[b.parity][at, :, j], q_sb[at, :, bass.ds(b.n * T, T)]
                                   ).then_inc(qblk_hi, 1)
                nc.scalar.copy(mask_now[:, b.parity], mask_bias[:, bass.ds(b.n * SC, SC)]
                               ).then_inc(mask_copied, 1)

            def keep_scores(b, g):
                if not (isinstance(b.n, int) and b.n == 0):
                    act.wait_ge(av_done, G * (b.n - 1) + g + 1)
                if g == 0:
                    act.wait_ge(mask_copied, b.n + 1)
                for c in range(SC):
                    act.wait_ge(s_in_psum, SC * (G * b.n + g) + c + 1)
                    nc.scalar.activation(probs[:, g, c], ps_s[:, c, 0:GT], ACT.Identity,
                                         bias=mask_now[:, b.parity, c:c + 1]).then_inc(s_kept, 1)

            def exponentials(b, g):
                act.wait_ge(shifted, G * b.n + g + 1)
                nc.scalar.activation(probs[:, g], probs[:, g], ACT.Exp,
                                     scale=scale).then_inc(probs_ready, 1)

            def keep_attn(b):
                act.wait_ge(av_done, G * b.n + G)
                if not (isinstance(b.n, int) and b.n == 0):
                    act.wait_ge(attnT_ready, b.n)
                for half in range(2):
                    at = slice(64 * half, 64 * half + OV)
                    nc.scalar.copy(attn_raw[at], ps_av[at, :, 0:G * T]).then_inc(attn_kept, 1)

            act.wait_ge(kb_ready, 1)
            act.wait_ge(mask_bias_ready, 1)
            act.wait_ge(pads_ready, 1)
            act.wait_ge(qblk_zeroed, 2)
            keep_nT_hi(batch(0), 0, DC - 1)
            block_q_hi(batch(0))
            for g in range(G):
                keep_k_hi(batch(0), g)

            def step(b, more, more2, prev):
                n = b.after(1)
                if more:
                    keep_nT_hi(n, 0, DC - 2)
                keep_scores(b, 0)
                if more:
                    keep_nT_hi(n, DC - 1, DC - 1)
                    keep_k_hi(n, 0)
                keep_scores(b, 1)
                if more:
                    keep_k_hi(n, 1)
                exponentials(b, 0)
                keep_scores(b, 2)
                if more:
                    keep_k_hi(n, 2)
                    block_q_hi(n)
                exponentials(b, 1)
                if more:
                    keep_k_hi(n, 3)
                keep_scores(b, 3)
                exponentials(b, 2)
                exponentials(b, 3)
                keep_attn(b)

            steps(act, step)

        @block.gpsimd
        def _(pool):
            nc.gpsimd.memset(ident[:], 0.0).then_inc(ident_ready, 1)
            pool.wait_ge(ident_ready, 1)
            nc.gpsimd.affine_select(out=ident[:], in_=ident[:], compare_op=ALU.not_equal, fill=1.0,
                                    base=0, pattern=[[-1, P]], channel_multiplier=1
                                    ).then_inc(ident_ready, 1)
            nc.gpsimd.memset(qblk_even[:].bitcast(F32), 0.0).then_inc(qblk_zeroed, 1)
            pool.wait_ge(xT_used, DC * QN)
            nc.gpsimd.memset(wqh[:].bitcast(F32), 0.0)
            nc.gpsimd.memset(wql[:].bitcast(F32), 0.0).then_inc(qblk_zeroed, 1)

            def row_maximum(b, g):
                if not (isinstance(b.n, int) and b.n == 0 and g < 2):
                    pool.wait_ge(shifted, G * b.n + g - 1)
                pool.wait_ge(colmax_ready, G * b.n + g + 1)
                pool.sem_inc(waited_pool, 1)
                nc.gpsimd.partition_all_reduce(rowmax[:, g % 2], colmax[:, g % 2], P,
                                               bass.bass_isa.ReduceOp.max).then_inc(rowmax_ready, 1)
                pool.wait_ge(rowmax_ready, G * b.n + g + 1)

            def step(b, more, more2, prev):
                for g in range(G):
                    row_maximum(b, g)

            steps(pool, step)

        @block.vector
        def _(dve):
            def layer_norm_stats(b):
                dve.wait_ge(ctx_in[b.parity], 32 * (b.pair + 1))
                for c in range(SC):
                    last = nc.vector.bn_stats(stats[0:rows[c], c], ctx_sb[0:rows[c], b.parity, c])
                last.then_inc(ln_step, 1)

            def layer_norm_rstd(b):
                base = LN_STEPS * b.n
                dve.wait_ge(ln_step, base + 1)
                dve.sem_inc(waited_dve, 1)
                for c in range(SC):
                    last = nc.vector.bn_aggr(mean_var[0:rows[c], c], stats[0:rows[c], c])
                last.then_inc(ln_step, 1)
                dve.wait_ge(ln_step, base + 2)
                nc.vector.tensor_scalar(var_eps[:], mean_var[:, :, 1], LN_EPS, None,
                                        ALU.add).then_inc(ln_step, 1)
                dve.wait_ge(ln_step, base + 3)
                nc.vector.tensor_scalar(half_bits[:], var_eps[:].bitcast(I32), 1, None,
                                        ALU.logical_shift_right).then_inc(ln_step, 1)
                dve.wait_ge(ln_step, base + 4)
                nc.vector.tensor_scalar(rstd[:].bitcast(I32), half_bits[:], -1.0, RSQRT_MAGIC,
                                        ALU.mult, ALU.add).then_inc(ln_step, 1)
                for k in range(NEWTON_STEPS):
                    dve.wait_ge(ln_step, base + 5 + 3 * k)
                    nc.vector.scalar_tensor_tensor(newton_a[:], rstd[:], -0.5, rstd[:], ALU.mult,
                                                   ALU.mult).then_inc(ln_step, 1)
                    dve.wait_ge(ln_step, base + 6 + 3 * k)
                    nc.vector.tensor_tensor(newton_b[:], newton_a[:], var_eps[:],
                                            ALU.mult).then_inc(ln_step, 1)
                    dve.wait_ge(ln_step, base + 7 + 3 * k)
                    nc.vector.scalar_tensor_tensor(rstd[:], newton_b[:], 1.5, rstd[:], ALU.add,
                                                   ALU.mult).then_inc(ln_step, 1)

            def layer_norm_apply(b):
                dve.wait_ge(ln_step, LN_STEPS * b.n + LN_STEPS)
                for c in range(SC):
                    at = ctx_sb[0:rows[c], b.parity, c]
                    last = nc.vector.tensor_scalar(at, at, mean_var[0:rows[c], c, 0:1],
                                                   rstd[0:rows[c], c:c + 1], ALU.subtract, ALU.mult)
                last.then_inc(normed, 1)

            def layer_norm(b):
                layer_norm_stats(b)
                layer_norm_rstd(b)
                layer_norm_apply(b)

            nc.vector.memset(ones[:], 1.0)
            nc.vector.memset(mean_var[:], 1.0).then_inc(setup, 1)
            nc.vector.memset(mask_f[:], 0.0).then_inc(setup, 1)
            nc.vector.memset(kTh[:, :, :, S:SC * P].bitcast(F32), 0.0)
            nc.vector.memset(kTl[:, :, :, S:SC * P].bitcast(F32), 0.0).then_inc(pads_ready, 1)
            dve.wait_ge(mask_in, 16)
            dve.wait_ge(setup, 2)
            nc.vector.tensor_copy(mask_f[:, 0:S], mask_u8[:]).then_inc(mask_cast, 1)

            def split_xT(i):
                for k in range(DC):
                    if i == 0:
                        dve.wait_ge(wq_hi, k + 1)
                        nc.vector.tensor_tensor(wql[:, k], wq_raw[:, k], wqh[:, k],
                                                ALU.subtract).then_inc(wq_lo, 1)
                    dve.wait_ge(xT_hi, DC * i + k + 1)
                    nc.vector.tensor_tensor(nTl[:, k], xT_raw[i % 2][:, k], nTh[:, k],
                                            ALU.subtract).then_inc(xT_lo, 1)

            split_xT(0)
            dve.wait_ge(maskT_in_psum, 1)
            by_batch = maskT[:].rearrange("p (c b) -> p b c", c=SC)
            biases = mask_bias[:].rearrange("p (b c) -> p b c", c=SC)
            nc.vector.tensor_copy(maskT[:], mask_bank[:, 0:SC * B]).then_inc(maskT_kept, 1)
            dve.wait_ge(maskT_kept, 1)
            nc.vector.tensor_scalar(biases, by_batch, 1.0, -MASKED, ALU.subtract, ALU.mult
                                    ).then_inc(setup, 1)
            dve.wait_ge(count_in_psum, 1)
            nc.vector.tensor_reduce(key_count[:], mask_bank[:, SC * B:2 * SC * B].rearrange(
                "p (c b) -> p b c", c=SC), mybir.AxisListType.X, ALU.add).then_inc(setup, 1)
            dve.wait_ge(setup, 4)
            nc.vector.reciprocal(key_count[:], key_count[:]).then_inc(setup, 1)
            dve.wait_ge(setup, 5)
            nc.vector.scalar_tensor_tensor(biases, key_count[:].unsqueeze(2).to_broadcast([P, B, SC]),
                                           0.0, biases, ALU.mult, ALU.add).then_inc(mask_bias_ready, 1)
            dve.wait_ge(ident_ready, 2)
            dve.wait_ge(small_in, 48)
            for k in range(DC):
                last = nc.vector.tensor_scalar(beta_bc[:, k], ident[:], 0.0, beta_sb[:, k:k + 1],
                                               ALU.mult, ALU.add)
            last.then_inc(beta_bc_ready, 1)
            split_xT(1)
            layer_norm(batch(0))
            for k in range(DC):
                dve.wait_ge(wk_hi, k + 1)
                nc.vector.scalar_tensor_tensor(wkl[:, k], wk_raw[:, k], gamma_sb[:, k:k + 1],
                                               wkh[:, k], ALU.mult, ALU.subtract).then_inc(wk_lo, 1)
            split_xT(2)
            for k in range(DC):
                dve.wait_ge(wv_hi, k + 1)
                nc.vector.scalar_tensor_tensor(wvl[:, k], wv_raw[:, k], gamma_sb[:, k:k + 1],
                                               wvh[:, k], ALU.mult, ALU.subtract).then_inc(wv_lo, 1)
            split_xT(3)
            dve.wait_ge(xT_lo, DC * QN)
            nc.vector.memset(v_sb[:, :, :, :, HEAD_DIM:HEAD_DIM + 1], 1.0).then_inc(setup, 1)
            layer_norm(batch(1))
            dve.wait_ge(kb_in_psum, 1)
            nc.vector.tensor_copy(k_bias[:], ps_s[:, 1, 0:G]).then_inc(kb_ready, 1)

            def block_q_lo(b):
                for j in range(HG):
                    at = slice(HEAD_DIM * j, HEAD_DIM * (j + 1))
                    dve.wait_ge(qblk_hi, HG * b.n + j + 1)
                    last = nc.vector.tensor_tensor(qblk_l[b.parity][at, :, j],
                                                   q_sb[at, :, bass.ds(b.n * T, T)],
                                                   qblk_h[b.parity][at, :, j], ALU.subtract)
                last.then_inc(qblk_ready, 1)

            def keep_nT_lo(b, first, last_chunk):
                for k in range(first, last_chunk + 1):
                    dve.wait_ge(nT_hi, DC * b.n + k + 1)
                    nc.vector.tensor_tensor(nTl[:, k, 0:S], ps_w[:, (U_NT + k) % 3, 0:S],
                                            nTh[:, k, 0:S], ALU.subtract).then_inc(drained, 1)

            def keep_k_lo(b, g):
                dve.wait_ge(k_hi, G * b.n + g + 1)
                nc.vector.scalar_tensor_tensor(kTl[:, b.parity, g, 0:S], ps_w[:, (U_K + g) % 3, 0:S],
                                               k_bias[:, g:g + 1], kTh[:, b.parity, g, 0:S],
                                               ALU.add, ALU.subtract).then_inc(drained, 1)

            def keep_v(b, c):
                dve.wait_ge(v_in_psum, SC * b.n + c + 1)
                nc.vector.tensor_tensor(
                    v_sb[0:rows[c], b.parity, c, :, 0:HEAD_DIM],
                    ps_w[0:rows[c], (U_V + c) % 3, :].rearrange("p (h d) -> p h d", h=H),
                    v_bias[0:rows[c]].rearrange("p (h d) -> p h d", h=H), ALU.add).then_inc(drained, 1)

            def column_maximum(b, g):
                dve.wait_ge(s_kept, SC * (G * b.n + g) + 2)
                nc.vector.tensor_tensor(colmax[:, g % 2], probs[:, g, 0], probs[:, g, 1],
                                        ALU.max).then_inc(max_partial, 1)
                dve.wait_ge(s_kept, SC * (G * b.n + g) + 3)
                dve.wait_ge(max_partial, G * b.n + g + 1)
                nc.vector.tensor_tensor(colmax[:, g % 2], colmax[:, g % 2], probs[:, g, 2],
                                        ALU.max).then_inc(colmax_ready, 1)

            def shift(b, g):
                dve.wait_ge(rowmax_ready, G * b.n + g + 1)
                nc.vector.tensor_tensor(probs[:, g], probs[:, g],
                                        rowmax[:, g % 2:g % 2 + 1].to_broadcast([P, SC, GT]),
                                        ALU.subtract).then_inc(shifted, 1)

            def invert_sums(b):
                dve.wait_ge(sums_in, 16 * b.n + 16)
                nc.vector.reciprocal(recips[:], sums[:]).then_inc(recips_ready, 1)

            def scale_attn(b):
                dve.wait_ge(recips_in, 32 * b.n + 32)
                if not (isinstance(b.n, int) and b.n == 0):
                    dve.wait_ge(out_in_psum, b.n)
                for slot in range(2):
                    for half in range(2):
                        j = 2 * slot + half
                        at = slice(64 * half, 64 * half + HEAD_DIM)
                        last = nc.vector.tensor_tensor(
                            attnT[HEAD_DIM * j:HEAD_DIM * (j + 1)].rearrange("p g t -> p (g t)"),
                            attn_raw[at, slot], recip_bc[at, slot], ALU.mult)
                last.then_inc(attnT_ready, 1)

            def gated_residual(b):
                dve.wait_ge(out_in_psum, b.n + 1)
                dve.wait_ge(x_in[b.parity], 16 * (b.pair + 1))
                if not (isinstance(b.n, int) and b.n == 0):
                    dve.wait_ge(stored, 16 * b.n)
                nc.vector.scalar_tensor_tensor(out_rows[0:T, b.parity], ps_w[0:T, U_OUT % 3, :],
                                               gate_sb[0:T, 1:2], x_rows[0:T, b.parity],
                                               ALU.mult, ALU.add).then_inc(out_ready, 1)

            dve.wait_ge(gate_ready, 1)
            keep_nT_lo(batch(0), 0, DC - 1)
            block_q_lo(batch(0))
            for g in range(G):
                keep_k_lo(batch(0), g)
            dve.wait_ge(vb_in_psum, 1)
            nc.vector.tensor_copy(v_bias[:], ps_s[:, 2, :]).then_inc(vb_ready, 1)
            dve.wait_ge(vb_ready, 1)
            dve.wait_ge(setup, 6)
            for c in range(SC):
                keep_v(batch(0), c)

            def step(b, more, more2, prev):
                n = b.after(1)
                if more:
                    keep_nT_lo(n, 0, DC - 2)
                column_maximum(b, 0)
                if more:
                    keep_nT_lo(n, DC - 1, DC - 1)
                    keep_k_lo(n, 0)
                if prev:
                    invert_sums(b.after(-1))
                column_maximum(b, 1)
                shift(b, 0)
                if more:
                    keep_k_lo(n, 1)
                column_maximum(b, 2)
                shift(b, 1)
                if more:
                    keep_k_lo(n, 2)
                if prev:
                    scale_attn(b.after(-1))
                if more:
                    keep_k_lo(n, 3)
                column_maximum(b, 3)
                shift(b, 2)
                if more:
                    block_q_lo(n)
                if more2:
                    layer_norm_stats(b.after(2))
                if more2:
                    layer_norm_rstd(b.after(2))
                shift(b, 3)
                if prev:
                    gated_residual(b.after(-1))
                if more2:
                    layer_norm_apply(b.after(2))
                if more:
                    for c in range(SC):
                        keep_v(n, c)

            steps(dve, step)
            invert_sums(batch(B - 1))
            scale_attn(batch(B - 1))
            gated_residual(batch(B - 1))


_INS = ["x", "xT", "ctx", "mask", "wqT", "wkT", "wvT", "woT", "gamma", "beta", "gate"]


def kernel(**inputs):
    import numpy as np
    import concourse.bacc as bacc
    from concourse.bass_utils import run_bass_kernel_spmd

    x = np.asarray(inputs["x"])
    B, T, D = x.shape
    laid = {
        "x": x,
        "xT": x.transpose(2, 0, 1).reshape(D, B * T),
        "ctx": np.asarray(inputs["ctx_2048"]),
        "mask": np.asarray(inputs["mask_BxS2_bf1"]).view(np.uint8),
        "wqT": np.asarray(inputs["L0_xattn_Wq"]).T,
        "wkT": np.asarray(inputs["L0_xattn_Wk"]).T,
        "wvT": np.asarray(inputs["L0_xattn_Wv"]).T,
        "woT": np.asarray(inputs["L0_xattn_Wo"]).T,
        "gamma": np.asarray(inputs["L0_xattn_ln_gamma"]).reshape(D // P, P).T,
        "beta": np.asarray(inputs["L0_xattn_ln_beta"]).reshape(D // P, P).T,
        "gate": np.asarray(inputs["L0_xattn_gate"]),
    }
    nc = bacc.Bacc("TRN2", target_bir_lowering=False, num_devices=1)
    arrays, args = {}, []
    for name in _INS:
        a = np.ascontiguousarray(laid[name])
        arrays["in_" + name] = a
        args.append(nc.dram_tensor("in_" + name, a.shape, mybir.dt.from_np(a.dtype),
                                   kind="ExternalInput").ap())
    args.append(nc.dram_tensor("out_rows_dram", (B, T, D), F32, kind="ExternalOutput").ap())
    xattn_program(nc, *args)
    r = run_bass_kernel_spmd(nc, [arrays], core_ids=[0])
    return r.results[0]["out_rows_dram"]
```

```python
from contextlib import ExitStack

import concourse.bass as bass
from concourse import mybir

F32 = mybir.dt.float32
F32R = mybir.dt.float32r
I32 = mybir.dt.int32
ALU = mybir.AluOpType
ACT = mybir.ActivationFunctionType

P = 128
HEAD_DIM = 32
LN_EPS = 1e-5
MASKED = -1e30
RSQRT_MAGIC = float(0x5F3759DF)
NEWTON_STEPS = 3
LN_STEPS = 5 + 3 * NEWTON_STEPS


class Batch:

    def __init__(self, n, parity, pair):
        self.n, self.parity, self.pair = n, parity, pair

    def after(self, k):
        p = self.parity + k
        return Batch(self.n + k, p % 2, self.pair + p // 2)


def batch(n):
    return Batch(n, n % 2, n // 2)


def xattn_program(nc, x, xT, ctx, mask, wqT, wkT, wvT, woT, gamma, beta, gate, out):
    B, T, D = x.shape
    S = ctx.shape[1]
    H = D // HEAD_DIM
    DC = D // P
    HG = P // HEAD_DIM
    G = H // HG
    SC = (S + P - 1) // P
    S_LAST = S - (SC - 1) * P
    S_EVEN = S + S % 2
    GT = HG * T
    QB = 4
    QN = B // QB
    QCOLS = QB * T
    VW = HEAD_DIM + 2
    OV = HEAD_DIM + 1
    U_NT, U_K, U_OUT, U_V = 0, DC, 2 * DC, 2 * DC + 1
    UNITS = 2 * DC + SC
    assert D == 512 and G == DC and SC == 3 and QCOLS <= 400 and GT <= 512 and B % QB == 0
    rows = [P] * (SC - 1) + [S_LAST]
    scale = HEAD_DIM ** -0.5

    sums_dram = nc.dram_tensor("sums_scratch", [2, H, T], F32, kind="Internal").ap()
    recip_dram = nc.dram_tensor("recip_scratch", [2, H, T], F32, kind="Internal").ap()

    with ExitStack() as stack:
        def sb(name, shape, dt=F32):
            return stack.enter_context(nc.sbuf_tensor(name, shape, dt))

        def sem(name):
            return stack.enter_context(nc.semaphore(name))

        ctx_sb = sb("ctx_sb", [P, 2, SC, D])
        nTh = sb("nTh", [P, DC, QCOLS], F32R)
        nTl = sb("nTl", [P, DC, QCOLS], F32R)
        wqh = sb("wqh", [P, DC, D], F32R)
        wql = sb("wql", [P, DC, D], F32R)
        wkh = sb("wkh", [P, DC, D], F32R)
        wkl = sb("wkl", [P, DC, D], F32R)
        wvh = sb("wvh", [P, DC, D], F32R)
        wvl = sb("wvl", [P, DC, D], F32R)
        woh = sb("woh", [P, DC, D], F32R)
        wol = sb("wol", [P, DC, D], F32R)
        q_sb = sb("q_sb", [P, G, B * T])
        kTh = sb("kTh", [P, 2, G, SC * P], F32R)
        kTl = sb("kTl", [P, 2, G, SC * P], F32R)
        v_sb = sb("v_sb", [P, 2, SC, H, VW])
        qblk_even = sb("qblk_even", [P, 2, G, HG, T], F32R)
        probs = sb("probs", [P, G, SC, GT])
        colmax = sb("colmax", [P, 2, GT])
        rowmax = sb("rowmax", [P, 2, GT])
        attn_raw = sb("attn_raw", [P, 2, G * T])
        recip_bc = sb("recip_bc", [P, 2, G * T])
        attnT = sb("attnT", [P, G, T])
        attnTh = sb("attnTh", [P, G, T], F32R)
        attnTl = sb("attnTl", [P, G, T], F32R)
        sums = sb("sums", [H, T])
        recips = sb("recips", [H, T])
        x_rows = sb("x_rows", [P, 2, D])
        ident = sb("ident", [P, P])
        mask_u8 = sb("mask_u8", [B, S], mybir.dt.uint8)
        mask_bias = sb("mask_bias", [P, B * SC])
        maskT = sb("maskT", [P, SC * B])
        ones = sb("ones", [P, P])
        key_count = sb("key_count", [P, B])
        mask_now = sb("mask_now", [P, 2, SC])
        gamma_sb = sb("gamma_sb", [P, DC])
        beta_sb = sb("beta_sb", [P, DC])
        k_bias = sb("k_bias", [P, G])
        v_bias = sb("v_bias", [P, D])
        gate_sb = sb("gate_sb", [P, 2])
        stats = sb("stats", [P, SC, 6])
        mean_var = sb("mean_var", [P, SC, 2])
        var_eps = sb("var_eps", [P, SC])
        half_bits = sb("half_bits", [P, SC], I32)
        rstd = sb("rstd", [P, SC])
        newton_a = sb("newton_a", [P, SC])
        newton_b = sb("newton_b", [P, SC])

        qblk_odd_h = wqh[:].rearrange("p a b -> p (a b)")[:, 0:G * GT].rearrange(
            "p (g j t) -> p g j t", g=G, j=HG)
        qblk_odd_l = wql[:].rearrange("p a b -> p (a b)")[:, 0:G * GT].rearrange(
            "p (g j t) -> p g j t", g=G, j=HG)
        qblk_h = [qblk_even[:, 0], qblk_odd_h]
        qblk_l = [qblk_even[:, 1], qblk_odd_l]
        probs_flat = probs[:].rearrange("p a c n -> p (a c n)")
        wq_raw, wv_raw = (probs_flat[:, i * DC * D:(i + 1) * DC * D].rearrange("p (k n) -> p k n", k=DC)
                          for i in range(2))
        wo_raw = wq_raw
        wk_raw = [attn_raw[:].rearrange("p a n -> p (a n)")[:, 0:D],
                  recip_bc[:].rearrange("p a n -> p (a n)")[:, 0:D], x_rows[:, 0], x_rows[:, 1]]
        beta_bc = colmax[:].rearrange("p a n -> p (a n)")[:, 0:DC * P].rearrange("p (k n) -> p k n", k=DC)
        mask_f = rowmax[:].rearrange("p a n -> p (a n)")[0:B, 0:SC * P]
        v_flat = v_sb[:].rearrange("p a c h w -> p (a c h w)")
        xT_raw = [v_flat[:, i * DC * QCOLS:(i + 1) * DC * QCOLS].rearrange("p (k n) -> p k n", k=DC)
                  for i in range(2)]

        ps_s = stack.enter_context(nc.psum_tensor("ps_s", [P, SC, 512], F32))
        ps_av = stack.enter_context(nc.psum_tensor("ps_av", [P, 2, 512], F32))
        ps_w = stack.enter_context(nc.psum_tensor("ps_w", [P, 3, 512], F32))
        mask_bank = ps_av[:, 1]
        q_banks = [[ps_s[:, 0], ps_s[:, 1], ps_s[:, 2], ps_w[:, 0]],
                   [ps_w[:, 1], ps_w[:, 2], ps_av[:, 0], ps_av[:, 1]]]

        def is_first(b):
            return isinstance(b.n, int) and b.n == 0

        def nT_bank(b, k):
            return q_banks[0][k] if is_first(b) else ps_w[:, (U_NT + k) % 3]

        last_banks = [ps_av[:, 0], ps_av[:, 1], ps_s[:, 0], ps_s[:, 1]]
        last_out = ps_s[:, 2]

        small_in = sem("small_in")
        mask_in = sem("mask_in")
        wq_in = [sem(f"wq_in{k}") for k in range(DC)]
        wk_in = [sem(f"wk_in{k}") for k in range(DC)]
        wv_in, wo_in = sem("wv_in"), sem("wo_in")
        xT_first = [sem(f"xT_first{k}") for k in range(DC)]
        xT_in = [sem("xT_in0"), sem("xT_in1")]
        ctx_in = [sem("ctx_in0"), sem("ctx_in1")]
        x_in = [sem("x_in0"), sem("x_in1")]
        ident_ready = sem("ident_ready")
        setup = sem("setup")
        mask_cast = sem("mask_cast")
        maskT_in_psum, mask_bias_ready = sem("maskT_in_psum"), sem("mask_bias_ready")
        maskT_kept, count_in_psum = sem("maskT_kept"), sem("count_in_psum")
        gate_ready = sem("gate_ready")
        wq_hi, wq_lo = sem("wq_hi"), sem("wq_lo")
        wk_hi, wk_lo = sem("wk_hi"), sem("wk_lo")
        wv_hi, wv_lo = sem("wv_hi"), sem("wv_lo")
        wo_hi, wo_lo = sem("wo_hi"), sem("wo_lo")
        xT_hi, xT_lo = sem("xT_hi"), sem("xT_lo")
        xT_used = sem("xT_used")
        q_in_psum, q_kept = sem("q_in_psum"), sem("q_kept")
        kb_in_psum, kb_ready = sem("kb_in_psum"), sem("kb_ready")
        vb_in_psum, vb_ready = sem("vb_in_psum"), sem("vb_ready")
        beta_bc_ready = sem("beta_bc_ready")
        qblk_zeroed = sem("qblk_zeroed")
        pads_ready = sem("pads_ready")
        mask_copied = sem("mask_copied")
        waited_dve, waited_pool = sem("waited_dve"), sem("waited_pool")
        ln_step = sem("ln_step")
        normed = sem("normed")
        nT_in_psum, k_in_psum, v_in_psum = sem("nT_in_psum"), sem("k_in_psum"), sem("v_in_psum")
        out_in_psum = sem("out_in_psum")
        nT_hi, k_hi = sem("nT_hi"), sem("k_hi")
        drained = sem("drained")
        qblk_hi, qblk_ready = sem("qblk_hi"), sem("qblk_ready")
        s_in_psum, s_kept = sem("s_in_psum"), sem("s_kept")
        max_partial, colmax_ready, rowmax_ready = sem("max_partial"), sem("colmax_ready"), sem("rowmax_ready")
        shifted, probs_ready, av_done = sem("shifted"), sem("probs_ready"), sem("av_done")
        attn_kept = sem("attn_kept")
        sums_out, sums_in = sem("sums_out"), sem("sums_in")
        recips_ready, recips_out, recips_in = sem("recips_ready"), sem("recips_out"), sem("recips_in")
        attnT_ready, attnT_hi, attnT_lo = sem("attnT_ready"), sem("attnT_hi"), sem("attnT_lo")
        out_ready = sem("out_ready")
        stored = sem("stored")
        last_inverted, last_scaled = sem("last_inverted"), sem("last_scaled")
        last_hi, last_split = sem("last_hi"), sem("last_split")

        block = stack.enter_context(nc.Block())

        def steps(engine, step):
            step(batch(0), True, True, False)
            step(batch(1), True, True, True)
            with engine.Fori(1, B // 2 - 1) as i:
                step(Batch(2 * i, 0, i), True, True, True)
                step(Batch(2 * i + 1, 1, i), True, True, True)
            step(batch(B - 2), True, False, True)
            step(batch(B - 1), False, False, True)

        @block.sync
        def _(sp):
            def load_ctx(b, again):
                if again:
                    sp.wait_ge(nT_in_psum, DC * (b.n - 1))
                sp.dma_start(ctx_sb[:, b.parity, 0:SC - 1],
                             ctx[b.n, 0:(SC - 1) * P].rearrange("(c p) d -> p c d", p=P)
                             ).then_inc(ctx_in[b.parity], 16)
                sp.dma_start(ctx_sb[0:S_LAST, b.parity, SC - 1],
                             ctx[b.n, (SC - 1) * P:S]).then_inc(ctx_in[b.parity], 16)

            def load_xT(i, again):
                if again:
                    sp.wait_ge(xT_lo, DC * (i - 1))
                sp.dma_start(xT_raw[i % 2], xT[:, i * QCOLS:(i + 1) * QCOLS].rearrange(
                    "(k p) n -> p k n", p=P)).then_inc(xT_in[i % 2], 16)

            def weights(w):
                return w.rearrange("(k p) n -> p k n", p=P)

            for k in range(DC):
                sp.dma_start(wq_raw[:, k], wqT[k * P:(k + 1) * P]).then_inc(wq_in[k], 16)
                sp.dma_start(xT_raw[0][:, k], xT[k * P:(k + 1) * P, 0:QCOLS]).then_inc(xT_first[k], 16)
                if k == 0:
                    sp.dma_start(mask_u8[:], mask).then_inc(mask_in, 16)
            load_xT(1, False)
            sp.dma_start(gamma_sb[:], gamma).then_inc(small_in, 16)
            sp.dma_start(beta_sb[:], beta).then_inc(small_in, 16)
            sp.dma_start(gate_sb[:, 0:1], gate[None, :].to_broadcast([P, 1])).then_inc(small_in, 16)
            load_ctx(batch(0), False)
            for k in range(DC):
                sp.dma_start(wk_raw[k], wkT[k * P:(k + 1) * P]).then_inc(wk_in[k], 16)
            load_ctx(batch(1), False)
            sp.dma_start(wv_raw, weights(wvT)).then_inc(wv_in, 16)
            for i in range(2, QN):
                load_xT(i, True)
            sp.dma_start(wo_raw, weights(woT)).then_inc(wo_in, 16)
            def load_x(b, again):
                if again:
                    sp.wait_ge(stored, 16 * (b.n - 1))
                sp.dma_start(x_rows[0:T, b.parity], x[b.n]).then_inc(x_in[b.parity], 16)

            sp.wait_ge(wk_lo, DC)
            sp.wait_ge(kb_in_psum, 1)
            load_x(batch(0), False)
            load_x(batch(1), False)

            def sums_round_trip(b):
                sp.wait_ge(attn_kept, 2 * b.n + 2)
                flat = sums_dram[b.parity].rearrange("(a s g) t -> a s (g t)", a=2, s=2)
                for half in range(2):
                    row = 64 * half + HEAD_DIM
                    sp.dma_start(flat[half:half + 1], attn_raw[row:row + 1]).then_inc(sums_out, 16)
                sp.wait_ge(sums_out, 32 * b.n + 32)
                sp.dma_start(sums[:], sums_dram[b.parity]).then_inc(sums_in, 16)
                sp.wait_ge(recips_ready, b.n + 1)
                sp.dma_start(recip_dram[b.parity], recips[:]).then_inc(recips_out, 16)
                sp.wait_ge(recips_out, 16 * b.n + 16)
                back = recip_dram[b.parity].rearrange("(a s g) t -> a (s g t)", a=2, s=2)
                for half in range(2):
                    lo = 64 * half
                    sp.dma_start(recip_bc[lo:lo + HEAD_DIM].rearrange("p a n -> p (a n)"),
                                 back[half:half + 1].to_broadcast([HEAD_DIM, 2 * G * T])
                                 ).then_inc(recips_in, 16)

            def store(b):
                sp.wait_ge(out_ready, b.n + 1)
                sp.dma_start(out[b.n], x_rows[0:T, b.parity]).then_inc(stored, 16)

            def step(b, more, more2, prev):
                if more2:
                    load_ctx(b.after(2), True)
                if prev:
                    sums_round_trip(b.after(-1))
                    store(b.after(-1))
                    if more:
                        load_x(b.after(1), True)

            steps(sp, step)
            last = batch(B - 1)
            store(last)
            sp.wait_ge(stored, 16 * B)

        @block.tensor
        def _(pe):
            def split_product(dst, wh, wl, mh, ml, start, stop):
                nc.tensor.matmul(dst, wh, mh, start=start, stop=False)
                nc.tensor.matmul(dst, wh, ml, start=False, stop=False)
                return nc.tensor.matmul(dst, wl, mh, start=False, stop=stop)

            pe.wait_ge(ident_ready, 2)
            pe.wait_ge(mask_cast, 1)
            for c in range(SC):
                last = nc.tensor.transpose(mask_bank[:, c * B:(c + 1) * B], mask_f[:, c * P:(c + 1) * P],
                                           ident[0:B, 0:B])
            last.then_inc(maskT_in_psum, 1)

            def bank_free(b, u):
                if not (isinstance(b.n, int) and UNITS * b.n + u - 2 <= 0):
                    pe.wait_ge(drained, UNITS * b.n + u - 2)

            def transposes(b, first, last_chunk):
                pe.wait_ge(normed, b.n + 1)
                for k in range(first, last_chunk + 1):
                    u = U_NT + k
                    if not is_first(b):
                        bank_free(b, u)
                    for c in range(SC):
                        last = nc.tensor.transpose(nT_bank(b, k)[:, c * P:c * P + rows[c]],
                                                   ctx_sb[0:rows[c], b.parity, c, k * P:(k + 1) * P],
                                                   ident[0:rows[c], 0:rows[c]])
                    last.then_inc(nT_in_psum, 1)

            for i in range(QN):
                for k in range(DC):
                    if i == 0:
                        pe.wait_ge(wq_lo, k + 1)
                    pe.wait_ge(xT_lo, DC * i + k + 1)
                    for g in range(G):
                        if k == 0 and i == 1 and g == G - 1:
                            pe.wait_ge(mask_bias_ready, 1)
                        if k == 0 and i >= 2:
                            pe.wait_ge(q_kept, G * (i - 2) + g + 1)
                        last = split_product(q_banks[i % 2][g][:, 0:QCOLS],
                                             wqh[:, k, g * P:(g + 1) * P], wql[:, k, g * P:(g + 1) * P],
                                             nTh[:, k], nTl[:, k], k == 0, k == DC - 1)
                        if k == DC - 1 and g < G - 1:
                            last.then_inc(q_in_psum, 1)
                    last.then_inc(xT_used, 1)
                    if i == 0 and k == 0:
                        pe.wait_ge(maskT_kept, 1)
                        nc.tensor.matmul(mask_bank[:, SC * B:2 * SC * B], ones[:], maskT[:],
                                         start=True, stop=True).then_inc(count_in_psum, 1)
                    elif i == QN - 1 and k == DC - 2:
                        pe.wait_ge(q_kept, G * (QN - 1))
                        transposes(batch(0), 0, DC - 1)
            def k_projection(b, g):
                u = U_K + g
                if is_first(b) and g < 2:
                    pe.wait_ge(q_kept, G * (QN - 1) + g + 1)
                if g:
                    pe.wait_ge(drained, UNITS * b.n + max(DC, u - 2))
                for k in range(DC):
                    if g == 0:
                        pe.wait_ge(drained, UNITS * b.n + max(k + 1, u - 2))
                    last = split_product(ps_w[:, u % 3, 0:S_EVEN],
                                         wkh[:, k, g * P:(g + 1) * P], wkl[:, k, g * P:(g + 1) * P],
                                         nTh[:, k, 0:S_EVEN], nTl[:, k, 0:S_EVEN], k == 0, k == DC - 1)
                last.then_inc(k_in_psum, 1)

            def v_projection(b, c):
                u = U_V + c
                if c < SC - 1:
                    pe.wait_ge(drained, UNITS * b.n + U_K + 3 + c)
                elif not (isinstance(b.n, int) and b.n < 2):
                    pe.wait_ge(out_ready, b.n - 1)
                for k in range(DC):
                    at = slice(c * P, c * P + rows[c])
                    last = split_product(ps_w[0:rows[c], u % 3, :], nTh[:, k, at], nTl[:, k, at],
                                         wvh[:, k], wvl[:, k], k == 0, k == DC - 1)
                last.then_inc(v_in_psum, 1)

            def scores(b, g):
                if g == 0:
                    pe.wait_ge(drained, UNITS * b.n + U_K + G)
                    pe.wait_ge(qblk_ready, b.n + 1)
                for c in range(SC):
                    if not (is_first(b) and g == 0):
                        pe.wait_ge(s_kept, SC * (G * b.n + g - 1) + c + 1)
                    at = slice(c * P, (c + 1) * P)
                    split_product(ps_s[:, c, 0:GT], kTh[:, b.parity, g, at], kTl[:, b.parity, g, at],
                                  qblk_h[b.parity][:, g], qblk_l[b.parity][:, g], True, True
                                  ).then_inc(s_in_psum, 1)

            def weighted_values(b, g):
                pe.wait_ge(probs_ready, G * b.n + g + 1)
                if g == 0:
                    pe.wait_ge(drained, UNITS * b.n + UNITS)
                    if not is_first(b):
                        pe.wait_ge(attn_kept, 2 * b.n)
                for slot in range(2):
                    for c in range(SC):
                        for half in range(2):
                            j = 2 * slot + half
                            last = nc.tensor.matmul(
                                ps_av[64 * half:64 * half + OV, slot, g * T:(g + 1) * T],
                                v_sb[0:rows[c], b.parity, c, HG * g + j, 0:OV],
                                probs[0:rows[c], g, c, j * T:(j + 1) * T],
                                start=c == 0, stop=c == SC - 1)
                last.then_inc(av_done, 1)

            def out_projection(b):
                pe.wait_ge(attnT_lo, b.n + 1)
                for g in range(G):
                    last = split_product(ps_w[0:T, U_OUT % 3, :], attnTh[:, g], attnTl[:, g],
                                         woh[:, g], wol[:, g], g == 0, g == G - 1)
                last.then_inc(out_in_psum, 1)

            pe.wait_ge(drained, 2)
            for g in range(G):
                for k in range(DC):
                    pe.wait_ge(wk_in[k], 16)
                    last = nc.tensor.matmul(ps_s[:, 1, g:g + 1], wk_raw[k][:, g * P:(g + 1) * P],
                                            beta_sb[:, k:k + 1], start=k == 0, stop=k == DC - 1)
            last.then_inc(kb_in_psum, 1)
            pe.wait_ge(wk_lo, DC)
            for g in range(G):
                k_projection(batch(0), g)
            pe.wait_ge(wv_in, 16)
            pe.wait_ge(beta_bc_ready, 1)
            for k in range(DC):
                last = nc.tensor.matmul(ps_s[:, 2, :], beta_bc[:, k], wv_raw[:, k], start=k == 0,
                                        stop=k == DC - 1)
            last.then_inc(vb_in_psum, 1)
            pe.wait_ge(wv_lo, DC)
            for c in range(SC):
                v_projection(batch(0), c)

            def previous_out_projection(b, u):
                pe.wait_ge(drained, UNITS * (b.n + 1) + u)
                out_projection(b.after(-1))

            def last_weighted_values(b, g):
                pe.wait_ge(probs_ready, G * b.n + g + 1)
                if g == 0:
                    pe.wait_ge(drained, UNITS * b.n + UNITS)
                    pe.wait_ge(attn_kept, 2 * b.n)
                elif g == 2:
                    pe.wait_ge(s_kept, SC * (G * b.n + G))
                bank = last_banks[g]
                by_half = probs[:, g].rearrange("p c (s a t) -> p c a s t", s=2, a=2)
                for half in range(2):
                    for c in range(SC):
                        nc.tensor.matmul(bank[64 * half:64 * half + 64, 2 * T:4 * T].rearrange(
                                             "p (s t) -> p s t", s=2),
                                         ones[0:rows[c], 0:64], by_half[0:rows[c], c, half],
                                         start=c == 0, stop=c == SC - 1)
                for slot in range(2):
                    for c in range(SC):
                        for half in range(2):
                            j = 2 * slot + half
                            last = nc.tensor.matmul(
                                bank[64 * half:64 * half + HEAD_DIM, slot * T:(slot + 1) * T],
                                v_sb[0:rows[c], b.parity, c, HG * g + j, 0:HEAD_DIM],
                                probs[0:rows[c], g, c, j * T:(j + 1) * T],
                                start=c == 0, stop=c == SC - 1)
                last.then_inc(av_done, 1)

            def last_out_projection(g):
                pe.wait_ge(last_split, g + 1)
                last = split_product(last_out[0:T], attnTh[:, g], attnTl[:, g], woh[:, g], wol[:, g],
                                     g == 0, g == G - 1)
                if g == G - 1:
                    last.then_inc(out_in_psum, 1)

            def step(b, more, more2, prev):
                n = b.after(1)
                if more:
                    transposes(n, 0, 1)
                scores(b, 0)
                if more:
                    transposes(n, 2, DC - 1)
                scores(b, 1)
                if more:
                    k_projection(n, 0)
                    k_projection(n, 1)
                scores(b, 2)
                if more:
                    k_projection(n, 2)
                    k_projection(n, 3)
                    weighted_values(b, 0)
                    scores(b, 3)
                    if more2:
                        v_projection(n, 0)
                    weighted_values(b, 1)
                    if more2:
                        v_projection(n, 1)
                    weighted_values(b, 2)
                    if prev:
                        previous_out_projection(b, U_K + 2)
                    weighted_values(b, 3)
                    if more2:
                        v_projection(n, 2)
                else:
                    v_projection(b, 0)
                    scores(b, 3)
                    v_projection(b, 1)
                    v_projection(b, 2)
                    last_weighted_values(b, 0)
                    last_weighted_values(b, 1)
                    previous_out_projection(b, 0)
                    last_weighted_values(b, 2)
                    last_weighted_values(b, 3)
                    for g in range(G):
                        last_out_projection(g)

            pe.wait_ge(vb_ready, 1)
            pe.wait_ge(kb_ready, 1)
            pe.wait_ge(wo_lo, DC)
            steps(pe, step)

        @block.scalar
        def _(act):
            def split_xT(i):
                for k in range(DC):
                    if i == 0:
                        act.wait_ge(wq_in[k], 16)
                        nc.scalar.copy(wqh[:, k], wq_raw[:, k]).then_inc(wq_hi, 1)
                        act.wait_ge(xT_first[k], 16)
                    elif k == 0:
                        act.wait_ge(xT_in[i % 2], 16 * ((i + 1) // 2))
                    if i >= 1:
                        act.wait_ge(xT_used, DC * (i - 1) + k + 1)
                    nc.scalar.copy(nTh[:, k], xT_raw[i % 2][:, k]).then_inc(xT_hi, 1)
                    if i == 2:
                        act.wait_ge(wk_in[k], 16)
                        nc.scalar.activation(wkh[:, k], wk_raw[k], ACT.Identity,
                                             scale=gamma_sb[:, k:k + 1]).then_inc(wk_hi, 1)
                    elif i == 3:
                        act.wait_ge(wv_in, 16)
                        nc.scalar.activation(wvh[:, k], wv_raw[:, k], ACT.Identity,
                                             scale=gamma_sb[:, k:k + 1]).then_inc(wv_hi, 1)

            def keep_q(i):
                for g in range(G):
                    if g < G - 1:
                        act.wait_ge(q_in_psum, (G - 1) * i + g + 1)
                    else:
                        act.wait_ge(xT_used, DC * (i + 1))
                    nc.scalar.copy(q_sb[:, g, i * QCOLS:(i + 1) * QCOLS],
                                   q_banks[i % 2][g][:, 0:QCOLS]).then_inc(q_kept, 1)

            split_xT(0)
            act.wait_ge(small_in, 48)
            nc.scalar.activation(gate_sb[:, 1:2], gate_sb[:, 0:1], ACT.Tanh).then_inc(gate_ready, 1)
            split_xT(1)
            keep_q(0)
            split_xT(2)
            keep_q(1)
            split_xT(3)
            keep_q(2)
            act.wait_ge(wo_in, 16)
            for k in range(DC):
                nc.scalar.copy(woh[:, k], wo_raw[:, k]).then_inc(wo_hi, 1)

            def keep_nT_hi(b, first, last_chunk):
                for k in range(first, last_chunk + 1):
                    act.wait_ge(nT_in_psum, DC * b.n + k + 1)
                    if is_first(b):
                        act.wait_ge(xT_used, DC * (QN - 1) + k + 1)
                    nc.scalar.copy(nTh[:, k, 0:S], nT_bank(b, k)[:, 0:S]).then_inc(nT_hi, 1)

            def keep_k_hi(b, g):
                act.wait_ge(k_in_psum, G * b.n + g + 1)
                nc.scalar.activation(kTh[:, b.parity, g, 0:S], ps_w[:, (U_K + g) % 3, 0:S],
                                     ACT.Identity, bias=k_bias[:, g:g + 1]).then_inc(k_hi, 1)

            def block_q_hi(b):
                for j in range(HG):
                    at = slice(HEAD_DIM * j, HEAD_DIM * (j + 1))
                    nc.scalar.copy(qblk_h[b.parity][at, :, j], q_sb[at, :, bass.ds(b.n * T, T)]
                                   ).then_inc(qblk_hi, 1)
                nc.scalar.copy(mask_now[:, b.parity], mask_bias[:, bass.ds(b.n * SC, SC)]
                               ).then_inc(mask_copied, 1)

            def keep_scores(b, g):
                if not is_first(b):
                    act.wait_ge(av_done, G * (b.n - 1) + g + 1)
                if g == 0:
                    act.wait_ge(mask_copied, b.n + 1)
                for c in range(SC):
                    act.wait_ge(s_in_psum, SC * (G * b.n + g) + c + 1)
                    nc.scalar.activation(probs[:, g, c], ps_s[:, c, 0:GT], ACT.Identity,
                                         bias=mask_now[:, b.parity, c:c + 1]).then_inc(s_kept, 1)

            def exponentials(b, g):
                act.wait_ge(shifted, G * b.n + g + 1)
                nc.scalar.activation(probs[:, g], probs[:, g], ACT.Exp,
                                     scale=scale).then_inc(probs_ready, 1)

            def split_attn_hi(b):
                act.wait_ge(attnT_ready, b.n + 1)
                nc.scalar.copy(attnTh[:], attnT[:]).then_inc(attnT_hi, 1)

            def keep_attn(b):
                act.wait_ge(av_done, G * b.n + G)
                if not is_first(b):
                    act.wait_ge(attnT_ready, b.n)
                for half in range(2):
                    at = slice(64 * half, 64 * half + OV)
                    nc.scalar.copy(attn_raw[at], ps_av[at, :, 0:G * T]).then_inc(attn_kept, 1)

            keep_nT_hi(batch(0), 0, DC - 1)
            keep_q(3)
            act.wait_ge(mask_bias_ready, 1)
            act.wait_ge(pads_ready, 1)
            act.wait_ge(qblk_zeroed, 2)
            block_q_hi(batch(0))
            act.wait_ge(kb_ready, 1)
            for g in range(G):
                keep_k_hi(batch(0), g)

            def step(b, more, more2, prev):
                n = b.after(1)
                if more:
                    keep_nT_hi(n, 0, 1)
                keep_scores(b, 0)
                if more:
                    keep_nT_hi(n, 2, DC - 1)
                keep_scores(b, 1)
                if more:
                    keep_k_hi(n, 0)
                    keep_k_hi(n, 1)
                keep_scores(b, 2)
                exponentials(b, 0)
                if more:
                    keep_k_hi(n, 2)
                    keep_k_hi(n, 3)
                keep_scores(b, 3)
                exponentials(b, 1)
                if prev:
                    split_attn_hi(b.after(-1))
                if more:
                    block_q_hi(n)
                exponentials(b, 2)
                exponentials(b, 3)
                if more:
                    keep_attn(b)

            steps(act, step)
            for g in range(G):
                act.wait_ge(last_scaled, g + 1)
                nc.scalar.copy(attnTh[:, g], attnT[:, g]).then_inc(last_hi, 1)

        @block.gpsimd
        def _(pool):
            nc.gpsimd.memset(ident[:], 0.0).then_inc(ident_ready, 1)
            pool.wait_ge(ident_ready, 1)
            nc.gpsimd.affine_select(out=ident[:], in_=ident[:], compare_op=ALU.not_equal, fill=1.0,
                                    base=0, pattern=[[-1, P]], channel_multiplier=1
                                    ).then_inc(ident_ready, 1)
            nc.gpsimd.memset(qblk_even[:].bitcast(F32), 0.0).then_inc(qblk_zeroed, 1)
            pool.wait_ge(xT_used, DC * QN)
            nc.gpsimd.memset(wqh[:].bitcast(F32), 0.0)
            nc.gpsimd.memset(wql[:].bitcast(F32), 0.0).then_inc(qblk_zeroed, 1)

            def row_maximum(b, g):
                if not (is_first(b) and g < 2):
                    pool.wait_ge(shifted, G * b.n + g - 1)
                pool.wait_ge(colmax_ready, G * b.n + g + 1)
                pool.sem_inc(waited_pool, 1)
                nc.gpsimd.partition_all_reduce(rowmax[:, g % 2], colmax[:, g % 2], P,
                                               bass.bass_isa.ReduceOp.max).then_inc(rowmax_ready, 1)
                pool.wait_ge(rowmax_ready, G * b.n + g + 1)

            def step(b, more, more2, prev):
                for g in range(G):
                    row_maximum(b, g)

            steps(pool, step)

        @block.vector
        def _(dve):
            def layer_norm_stats(b):
                dve.wait_ge(ctx_in[b.parity], 32 * (b.pair + 1))
                for c in range(SC):
                    last = nc.vector.bn_stats(stats[0:rows[c], c], ctx_sb[0:rows[c], b.parity, c])
                last.then_inc(ln_step, 1)

            def layer_norm_rstd(b):
                base = LN_STEPS * b.n
                dve.wait_ge(ln_step, base + 1)
                dve.sem_inc(waited_dve, 1)
                for c in range(SC):
                    last = nc.vector.bn_aggr(mean_var[0:rows[c], c], stats[0:rows[c], c])
                last.then_inc(ln_step, 1)
                dve.wait_ge(ln_step, base + 2)
                nc.vector.tensor_scalar(var_eps[:], mean_var[:, :, 1], LN_EPS, None,
                                        ALU.add).then_inc(ln_step, 1)
                dve.wait_ge(ln_step, base + 3)
                nc.vector.tensor_scalar(half_bits[:], var_eps[:].bitcast(I32), 1, None,
                                        ALU.logical_shift_right).then_inc(ln_step, 1)
                dve.wait_ge(ln_step, base + 4)
                nc.vector.tensor_scalar(rstd[:].bitcast(I32), half_bits[:], -1.0, RSQRT_MAGIC,
                                        ALU.mult, ALU.add).then_inc(ln_step, 1)
                for k in range(NEWTON_STEPS):
                    dve.wait_ge(ln_step, base + 5 + 3 * k)
                    nc.vector.scalar_tensor_tensor(newton_a[:], rstd[:], -0.5, rstd[:], ALU.mult,
                                                   ALU.mult).then_inc(ln_step, 1)
                    dve.wait_ge(ln_step, base + 6 + 3 * k)
                    nc.vector.tensor_tensor(newton_b[:], newton_a[:], var_eps[:],
                                            ALU.mult).then_inc(ln_step, 1)
                    dve.wait_ge(ln_step, base + 7 + 3 * k)
                    nc.vector.scalar_tensor_tensor(rstd[:], newton_b[:], 1.5, rstd[:], ALU.add,
                                                   ALU.mult).then_inc(ln_step, 1)

            def layer_norm_apply(b):
                dve.wait_ge(ln_step, LN_STEPS * b.n + LN_STEPS)
                for c in range(SC):
                    at = ctx_sb[0:rows[c], b.parity, c]
                    last = nc.vector.tensor_scalar(at, at, mean_var[0:rows[c], c, 0:1],
                                                   rstd[0:rows[c], c:c + 1], ALU.subtract, ALU.mult)
                last.then_inc(normed, 1)

            def layer_norm(b):
                layer_norm_stats(b)
                layer_norm_rstd(b)
                layer_norm_apply(b)

            nc.vector.memset(ones[:], 1.0)
            nc.vector.memset(mean_var[:], 1.0).then_inc(setup, 1)
            nc.vector.memset(mask_f, 0.0).then_inc(setup, 1)
            dve.wait_ge(mask_in, 16)
            dve.wait_ge(setup, 2)
            nc.vector.tensor_copy(mask_f[:, 0:S], mask_u8[:]).then_inc(mask_cast, 1)

            def split_xT(i):
                for k in range(DC):
                    if i == 0:
                        dve.wait_ge(wq_hi, k + 1)
                        nc.vector.tensor_tensor(wql[:, k], wq_raw[:, k], wqh[:, k],
                                                ALU.subtract).then_inc(wq_lo, 1)
                    dve.wait_ge(xT_hi, DC * i + k + 1)
                    nc.vector.tensor_tensor(nTl[:, k], xT_raw[i % 2][:, k], nTh[:, k],
                                            ALU.subtract).then_inc(xT_lo, 1)
                    if i == 0 and k == 0:
                        dve.wait_ge(maskT_in_psum, 1)
                        nc.vector.tensor_copy(maskT[:], mask_bank[:, 0:SC * B]).then_inc(maskT_kept, 1)
                    if i == 2:
                        dve.wait_ge(wk_hi, k + 1)
                        nc.vector.scalar_tensor_tensor(wkl[:, k], wk_raw[k], gamma_sb[:, k:k + 1],
                                                       wkh[:, k], ALU.mult, ALU.subtract
                                                       ).then_inc(wk_lo, 1)
                    elif i == 3:
                        dve.wait_ge(wv_hi, k + 1)
                        nc.vector.scalar_tensor_tensor(wvl[:, k], wv_raw[:, k], gamma_sb[:, k:k + 1],
                                                       wvh[:, k], ALU.mult, ALU.subtract
                                                       ).then_inc(wv_lo, 1)

            split_xT(0)
            by_batch = maskT[:].rearrange("p (c b) -> p b c", c=SC)
            biases = mask_bias[:].rearrange("p (b c) -> p b c", c=SC)
            dve.wait_ge(maskT_kept, 1)
            nc.vector.tensor_scalar(biases, by_batch, 1.0, -MASKED, ALU.subtract, ALU.mult
                                    ).then_inc(setup, 1)
            dve.wait_ge(count_in_psum, 1)
            nc.vector.tensor_reduce(key_count[:], mask_bank[:, SC * B:2 * SC * B].rearrange(
                "p (c b) -> p b c", c=SC), mybir.AxisListType.X, ALU.add).then_inc(setup, 1)
            dve.wait_ge(setup, 4)
            nc.vector.reciprocal(key_count[:], key_count[:]).then_inc(setup, 1)
            dve.wait_ge(setup, 5)
            nc.vector.scalar_tensor_tensor(biases, key_count[:].unsqueeze(2).to_broadcast([P, B, SC]),
                                           0.0, biases, ALU.mult, ALU.add).then_inc(mask_bias_ready, 1)
            dve.wait_ge(ident_ready, 2)
            dve.wait_ge(small_in, 48)
            for k in range(DC):
                last = nc.vector.tensor_scalar(beta_bc[:, k], ident[:], 0.0, beta_sb[:, k:k + 1],
                                               ALU.mult, ALU.add)
            last.then_inc(beta_bc_ready, 1)
            split_xT(1)
            layer_norm(batch(0))
            split_xT(2)
            split_xT(3)
            dve.wait_ge(wk_lo, DC)
            nc.vector.memset(kTh[:, :, :, S:SC * P].bitcast(F32), 0.0)
            nc.vector.memset(kTl[:, :, :, S:SC * P].bitcast(F32), 0.0).then_inc(pads_ready, 1)
            dve.wait_ge(xT_lo, DC * QN)
            nc.vector.memset(v_sb[:, :, :, :, HEAD_DIM:HEAD_DIM + 1], 1.0).then_inc(setup, 1)
            for k in range(DC):
                dve.wait_ge(wo_hi, k + 1)
                nc.vector.tensor_tensor(wol[:, k], wo_raw[:, k], woh[:, k], ALU.subtract).then_inc(wo_lo, 1)
            def block_q_lo(b):
                for j in range(HG):
                    at = slice(HEAD_DIM * j, HEAD_DIM * (j + 1))
                    dve.wait_ge(qblk_hi, HG * b.n + j + 1)
                    last = nc.vector.tensor_tensor(qblk_l[b.parity][at, :, j],
                                                   q_sb[at, :, bass.ds(b.n * T, T)],
                                                   qblk_h[b.parity][at, :, j], ALU.subtract)
                last.then_inc(qblk_ready, 1)

            def keep_nT_lo(b, first, last_chunk):
                for k in range(first, last_chunk + 1):
                    dve.wait_ge(nT_hi, DC * b.n + k + 1)
                    nc.vector.tensor_tensor(nTl[:, k, 0:S], nT_bank(b, k)[:, 0:S],
                                            nTh[:, k, 0:S], ALU.subtract).then_inc(drained, 1)

            def keep_k_lo(b, g):
                dve.wait_ge(k_hi, G * b.n + g + 1)
                nc.vector.scalar_tensor_tensor(kTl[:, b.parity, g, 0:S], ps_w[:, (U_K + g) % 3, 0:S],
                                               k_bias[:, g:g + 1], kTh[:, b.parity, g, 0:S],
                                               ALU.add, ALU.subtract).then_inc(drained, 1)

            def keep_v(b, c):
                dve.wait_ge(v_in_psum, SC * b.n + c + 1)
                nc.vector.tensor_tensor(
                    v_sb[0:rows[c], b.parity, c, :, 0:HEAD_DIM],
                    ps_w[0:rows[c], (U_V + c) % 3, :].rearrange("p (h d) -> p h d", h=H),
                    v_bias[0:rows[c]].rearrange("p (h d) -> p h d", h=H), ALU.add).then_inc(drained, 1)

            def column_maximum(b, g):
                dve.wait_ge(s_kept, SC * (G * b.n + g) + 2)
                nc.vector.tensor_tensor(colmax[:, g % 2], probs[:, g, 0], probs[:, g, 1],
                                        ALU.max).then_inc(max_partial, 1)
                dve.wait_ge(s_kept, SC * (G * b.n + g) + 3)
                dve.wait_ge(max_partial, G * b.n + g + 1)
                nc.vector.tensor_tensor(colmax[:, g % 2], colmax[:, g % 2], probs[:, g, 2],
                                        ALU.max).then_inc(colmax_ready, 1)

            def shift(b, g):
                dve.wait_ge(rowmax_ready, G * b.n + g + 1)
                nc.vector.tensor_tensor(probs[:, g], probs[:, g],
                                        rowmax[:, g % 2:g % 2 + 1].to_broadcast([P, SC, GT]),
                                        ALU.subtract).then_inc(shifted, 1)

            def invert_sums(b):
                dve.wait_ge(sums_in, 16 * b.n + 16)
                nc.vector.reciprocal(recips[:], sums[:]).then_inc(recips_ready, 1)

            def scale_attn(b):
                dve.wait_ge(recips_in, 32 * b.n + 32)
                if not is_first(b):
                    dve.wait_ge(out_in_psum, b.n)
                for slot in range(2):
                    for half in range(2):
                        j = 2 * slot + half
                        at = slice(64 * half, 64 * half + HEAD_DIM)
                        last = nc.vector.tensor_tensor(
                            attnT[HEAD_DIM * j:HEAD_DIM * (j + 1)].rearrange("p g t -> p (g t)"),
                            attn_raw[at, slot], recip_bc[at, slot], ALU.mult)
                last.then_inc(attnT_ready, 1)

            def split_attn_lo(b):
                dve.wait_ge(attnT_hi, b.n + 1)
                nc.vector.tensor_tensor(attnTl[:], attnT[:], attnTh[:], ALU.subtract
                                        ).then_inc(attnT_lo, 1)

            def gated_residual(b, bank):
                dve.wait_ge(out_in_psum, b.n + 1)
                dve.wait_ge(x_in[b.parity], 16 * (b.pair + 1))
                nc.vector.scalar_tensor_tensor(x_rows[0:T, b.parity], bank[0:T],
                                               gate_sb[0:T, 1:2], x_rows[0:T, b.parity],
                                               ALU.mult, ALU.add).then_inc(out_ready, 1)

            dve.wait_ge(gate_ready, 1)
            first, second = batch(0), batch(1)
            keep_nT_lo(first, 0, DC - 1)
            block_q_lo(first)
            dve.wait_ge(kb_in_psum, 1)
            nc.vector.tensor_copy(k_bias[:], ps_s[:, 1, 0:G]).then_inc(kb_ready, 1)
            dve.wait_ge(kb_ready, 1)
            keep_k_lo(first, 0)
            keep_k_lo(first, 1)
            layer_norm_stats(second)
            keep_k_lo(first, 2)
            keep_k_lo(first, 3)
            layer_norm_rstd(second)
            dve.wait_ge(vb_in_psum, 1)
            nc.vector.tensor_copy(v_bias[:], ps_s[:, 2, :]).then_inc(vb_ready, 1)
            dve.wait_ge(vb_ready, 1)
            dve.wait_ge(setup, 6)
            keep_v(first, 0)
            layer_norm_apply(second)
            keep_v(first, 1)
            keep_v(first, 2)

            def last_invert(g):
                dve.wait_ge(av_done, G * (B - 1) + g + 1)
                nc.vector.reciprocal(recip_bc[:, :, g * T:(g + 1) * T], last_banks[g][:, 2 * T:4 * T]
                                     .rearrange("p (s t) -> p s t", s=2)).then_inc(last_inverted, 1)

            def last_scale(g):
                dve.wait_ge(last_inverted, g + 1)
                for slot in range(2):
                    for half in range(2):
                        j = 2 * slot + half
                        at = slice(64 * half, 64 * half + HEAD_DIM)
                        last = nc.vector.tensor_tensor(attnT[HEAD_DIM * j:HEAD_DIM * (j + 1), g],
                                                       last_banks[g][at, slot * T:(slot + 1) * T],
                                                       recip_bc[at, slot, g * T:(g + 1) * T], ALU.mult)
                last.then_inc(last_scaled, 1)

            def last_split_lo(g):
                dve.wait_ge(last_hi, g + 1)
                nc.vector.tensor_tensor(attnTl[:, g], attnT[:, g], attnTh[:, g], ALU.subtract
                                        ).then_inc(last_split, 1)

            def step(b, more, more2, prev):
                n = b.after(1)
                if more:
                    keep_nT_lo(n, 0, DC - 1)
                if prev:
                    invert_sums(b.after(-1))
                column_maximum(b, 0)
                column_maximum(b, 1)
                if more:
                    keep_k_lo(n, 0)
                    keep_k_lo(n, 1)
                shift(b, 0)
                if not more:
                    keep_v(b, 0)
                column_maximum(b, 2)
                shift(b, 1)
                if more:
                    keep_k_lo(n, 2)
                else:
                    keep_v(b, 1)
                if prev:
                    scale_attn(b.after(-1))
                column_maximum(b, 3)
                if more:
                    keep_k_lo(n, 3)
                else:
                    keep_v(b, 2)
                shift(b, 2)
                if prev:
                    split_attn_lo(b.after(-1))
                if more:
                    block_q_lo(n)
                if more2:
                    keep_v(n, 0)
                shift(b, 3)
                if more2:
                    layer_norm_stats(b.after(2))
                if not more:
                    last_invert(0)
                    last_invert(1)
                if prev:
                    gated_residual(b.after(-1), ps_w[:, U_OUT % 3])
                if more2:
                    layer_norm_rstd(b.after(2))
                    keep_v(n, 1)
                    layer_norm_apply(b.after(2))
                    keep_v(n, 2)

            steps(dve, step)
            last_scale(0)
            last_scale(1)
            last_split_lo(0)
            last_invert(2)
            last_scale(2)
            last_split_lo(1)
            last_invert(3)
            last_scale(3)
            last_split_lo(2)
            last_split_lo(3)
            gated_residual(batch(B - 1), last_out)


_INS = ["x", "xT", "ctx", "mask", "wqT", "wkT", "wvT", "woT", "gamma", "beta", "gate"]


def kernel(**inputs):
    import numpy as np
    import concourse.bacc as bacc
    from concourse.bass_utils import run_bass_kernel_spmd

    x = np.asarray(inputs["x"])
    B, T, D = x.shape
    laid = {
        "x": x,
        "xT": x.transpose(2, 0, 1).reshape(D, B * T),
        "ctx": np.asarray(inputs["ctx_2048"]),
        "mask": np.asarray(inputs["mask_BxS2_bf1"]).view(np.uint8),
        "wqT": np.asarray(inputs["L0_xattn_Wq"]).T,
        "wkT": np.asarray(inputs["L0_xattn_Wk"]).T,
        "wvT": np.asarray(inputs["L0_xattn_Wv"]).T,
        "woT": np.asarray(inputs["L0_xattn_Wo"]).T,
        "gamma": np.asarray(inputs["L0_xattn_ln_gamma"]).reshape(D // P, P).T,
        "beta": np.asarray(inputs["L0_xattn_ln_beta"]).reshape(D // P, P).T,
        "gate": np.asarray(inputs["L0_xattn_gate"]),
    }
    nc = bacc.Bacc("TRN2", target_bir_lowering=False, num_devices=1)
    arrays, args = {}, []
    for name in _INS:
        a = np.ascontiguousarray(laid[name])
        arrays["in_" + name] = a
        args.append(nc.dram_tensor("in_" + name, a.shape, mybir.dt.from_np(a.dtype),
                                   kind="ExternalInput").ap())
    args.append(nc.dram_tensor("out_rows_dram", (B, T, D), F32, kind="ExternalOutput").ap())
    xattn_program(nc, *args)
    r = run_bass_kernel_spmd(nc, [arrays], core_ids=[0])
    return r.results[0]["out_rows_dram"]
```

```python
from contextlib import ExitStack

import concourse.bass as bass
from concourse import mybir

F32 = mybir.dt.float32
F32R = mybir.dt.float32r
I32 = mybir.dt.int32
ALU = mybir.AluOpType
ACT = mybir.ActivationFunctionType

P = 128
HEAD_DIM = 32
LN_EPS = 1e-5
MASKED = -1e30
RSQRT_MAGIC = float(0x5F3759DF)
NEWTON_STEPS = 3
RSTD_STEPS = 4 + 3 * NEWTON_STEPS
LN_STEPS = 1 + RSTD_STEPS


class Batch:

    def __init__(self, n, parity, pair):
        self.n, self.parity, self.pair = n, parity, pair

    def after(self, k):
        p = self.parity + k
        return Batch(self.n + k, p % 2, self.pair + p // 2)


def batch(n):
    return Batch(n, n % 2, n // 2)


def xattn_program(nc, x, xT, ctx, mask, wqT, wkT, wvT, woT, gamma, beta, gate, out):
    B, T, D = x.shape
    S = ctx.shape[1]
    H = D // HEAD_DIM
    DC = D // P
    HG = P // HEAD_DIM
    G = H // HG
    SC = (S + P - 1) // P
    S_LAST = S - (SC - 1) * P
    S_EVEN = S + S % 2
    GT = HG * T
    QB = 4
    QN = B // QB
    QCOLS = QB * T
    OV = HEAD_DIM + 1
    VW = HEAD_DIM + 2
    U_NT, U_K, U_OUT, U_V = 0, DC, 2 * DC, 2 * DC + 1
    UNITS = 2 * DC + SC
    assert D == 512 and G == DC and SC == 3 and QCOLS <= 400 and GT <= 512 and B % QB == 0
    rows = [P] * (SC - 1) + [S_LAST]
    scale = HEAD_DIM ** -0.5

    sums_dram = nc.dram_tensor("sums_scratch", [2, H, T], F32, kind="Internal").ap()
    recip_dram = nc.dram_tensor("recip_scratch", [2, H, T], F32, kind="Internal").ap()

    with ExitStack() as stack:
        def sb(name, shape, dt=F32):
            return stack.enter_context(nc.sbuf_tensor(name, shape, dt))

        def sem(name):
            return stack.enter_context(nc.semaphore(name))

        ctx_sb = sb("ctx_sb", [P, 2, SC, D])
        nTh = sb("nTh", [P, DC, QCOLS], F32R)
        nTl = sb("nTl", [P, DC, QCOLS], F32R)
        wqh = sb("wqh", [P, DC, D], F32R)
        wql = sb("wql", [P, DC, D], F32R)
        wkh = sb("wkh", [P, DC, D], F32R)
        wkl = sb("wkl", [P, DC, D], F32R)
        wvh = sb("wvh", [P, DC, D], F32R)
        wvl = sb("wvl", [P, DC, D], F32R)
        woh = sb("woh", [P, DC, D], F32R)
        wol = sb("wol", [P, DC, D], F32R)
        q_sb = sb("q_sb", [P, G, B * T])
        kTh = sb("kTh", [P, 2, G, SC * P], F32R)
        kTl = sb("kTl", [P, 2, G, SC * P], F32R)
        v_sb = sb("v_sb", [P, 2, SC, H, VW])
        qblk_even = sb("qblk_even", [P, 2, G, HG, T], F32R)
        probs = sb("probs", [P, G, SC, GT])
        colmax = sb("colmax", [P, 2, GT])
        rowmax = sb("rowmax", [P, 2, GT])
        attn_raw = sb("attn_raw", [P, 2, G * T])
        recip_bc = sb("recip_bc", [P, 2, G * T])
        sums = sb("sums", [H, T])
        recips = sb("recips", [H, T])
        attnT = sb("attnT", [P, G, T])
        attnTh = sb("attnTh", [P, G, T], F32R)
        attnTl = sb("attnTl", [P, G, T], F32R)
        x_rows = sb("x_rows", [P, 2, D])
        ident = sb("ident", [P, P])
        mask_u8 = sb("mask_u8", [B, S], mybir.dt.uint8)
        mask_bias = sb("mask_bias", [P, B * SC])
        maskT = sb("maskT", [P, SC * B])
        ones = sb("ones", [P, P])
        key_count = sb("key_count", [P, B])
        mask_now = sb("mask_now", [P, 2, SC])
        gamma_sb = sb("gamma_sb", [P, DC])
        beta_sb = sb("beta_sb", [P, DC])
        k_bias = sb("k_bias", [P, G])
        v_bias = sb("v_bias", [P, D])
        gate_sb = sb("gate_sb", [P, 2])
        stats = sb("stats", [P, SC, 6])
        mean_var = sb("mean_var", [P, SC, 2])
        var_eps = sb("var_eps", [P, SC])
        half_bits = sb("half_bits", [P, SC], I32)
        rstd = sb("rstd", [P, SC])
        newton_a = sb("newton_a", [P, SC])
        newton_b = sb("newton_b", [P, SC])

        qblk_odd_h = wqh[:].rearrange("p a b -> p (a b)")[:, 0:G * GT].rearrange(
            "p (g j t) -> p g j t", g=G, j=HG)
        qblk_odd_l = wql[:].rearrange("p a b -> p (a b)")[:, 0:G * GT].rearrange(
            "p (g j t) -> p g j t", g=G, j=HG)
        qblk_h = [qblk_even[:, 0], qblk_odd_h]
        qblk_l = [qblk_even[:, 1], qblk_odd_l]
        probs_flat = probs[:].rearrange("p a c n -> p (a c n)")
        wq_raw, wv_raw = (probs_flat[:, i * DC * D:(i + 1) * DC * D].rearrange("p (k n) -> p k n", k=DC)
                          for i in range(2))
        wo_raw = wq_raw
        wk_raw = [attn_raw[:].rearrange("p a n -> p (a n)")[:, 0:D],
                  recip_bc[:].rearrange("p a n -> p (a n)")[:, 0:D], x_rows[:, 0], x_rows[:, 1]]
        beta_bc = colmax[:].rearrange("p a n -> p (a n)")[:, 0:DC * P].rearrange("p (k n) -> p k n", k=DC)
        mask_f = rowmax[:].rearrange("p a n -> p (a n)")[0:B, 0:SC * P]
        v_flat = v_sb[:].rearrange("p a c h w -> p (a c h w)")
        xT_raw = [v_flat[:, i * DC * QCOLS:(i + 1) * DC * QCOLS].rearrange("p (k n) -> p k n", k=DC)
                  for i in range(2)]

        ps_s = stack.enter_context(nc.psum_tensor("ps_s", [P, SC, 512], F32))
        ps_av = stack.enter_context(nc.psum_tensor("ps_av", [P, 2, 512], F32))
        ps_w = stack.enter_context(nc.psum_tensor("ps_w", [P, 3, 512], F32))
        mask_bank = ps_av[:, 1]
        q_banks = [[ps_s[:, 0], ps_s[:, 1], ps_s[:, 2], ps_w[:, 0]],
                   [ps_w[:, 1], ps_w[:, 2], ps_av[:, 0], ps_av[:, 1]]]

        def is_first(b):
            return isinstance(b.n, int) and b.n == 0

        def nT_bank(b, k):
            return q_banks[0][k] if is_first(b) else ps_w[:, (U_NT + k) % 3]

        last_banks = [ps_av[:, 0], ps_av[:, 1], ps_s[:, 0], ps_s[:, 1]]

        def is_last(b):
            return isinstance(b.n, int) and b.n == B - 1

        last_attnTh, last_attnTl = (t[:, 0, 0:G * T].rearrange("p (g t) -> p g t", g=G)
                                    for t in (nTh, nTl))

        last_recip = colmax[:, 0]

        def out_bank(b):
            if is_last(b):
                return ps_s[:, 2]
            return ps_w[:, 0 if isinstance(b.n, int) and b.n == B - 2 else U_OUT % 3]

        small_in = sem("small_in")
        mask_in = sem("mask_in")
        wq_in = [sem(f"wq_in{k}") for k in range(DC)]
        wk_in = [sem(f"wk_in{k}") for k in range(DC)]
        wv_in, wo_in = sem("wv_in"), sem("wo_in")
        xT_first = [sem(f"xT_first{k}") for k in range(DC)]
        xT_in = [sem("xT_in0"), sem("xT_in1")]
        ctx_in = [sem("ctx_in0"), sem("ctx_in1")]
        x_in = [sem("x_in0"), sem("x_in1")]
        ident_ready = sem("ident_ready")
        setup = sem("setup")
        mask_cast = sem("mask_cast")
        maskT_in_psum, mask_bias_ready = sem("maskT_in_psum"), sem("mask_bias_ready")
        maskT_kept, count_in_psum = sem("maskT_kept"), sem("count_in_psum")
        gate_ready = sem("gate_ready")
        wq_hi, wq_lo = sem("wq_hi"), sem("wq_lo")
        wk_hi, wk_lo = sem("wk_hi"), sem("wk_lo")
        wv_hi, wv_lo = sem("wv_hi"), sem("wv_lo")
        wo_hi, wo_lo = sem("wo_hi"), sem("wo_lo")
        xT_hi, xT_lo = sem("xT_hi"), sem("xT_lo")
        xT_used = sem("xT_used")
        q_in_psum, q_kept = sem("q_in_psum"), sem("q_kept")
        kb_in_psum, kb_ready = sem("kb_in_psum"), sem("kb_ready")
        vb_in_psum, vb_ready = sem("vb_in_psum"), sem("vb_ready")
        beta_bc_ready = sem("beta_bc_ready")
        qblk_zeroed = sem("qblk_zeroed")
        pads_ready = sem("pads_ready")
        mask_copied = sem("mask_copied")
        waited_dve, waited_pool = sem("waited_dve"), sem("waited_pool")
        ln_step = sem("ln_step")
        normed = sem("normed")
        nT_in_psum, k_in_psum, v_in_psum = sem("nT_in_psum"), sem("k_in_psum"), sem("v_in_psum")
        out_in_psum = sem("out_in_psum")
        nT_hi, k_hi = sem("nT_hi"), sem("k_hi")
        drained = sem("drained")
        qblk_hi, qblk_ready = sem("qblk_hi"), sem("qblk_ready")
        s_in_psum, s_kept = sem("s_in_psum"), sem("s_kept")
        max_partial, colmax_ready, rowmax_ready = sem("max_partial"), sem("colmax_ready"), sem("rowmax_ready")
        shifted, probs_ready, av_done = sem("shifted"), sem("probs_ready"), sem("av_done")
        attn_kept = sem("attn_kept")
        sums_out, sums_in = sem("sums_out"), sem("sums_in")
        recips_ready, recips_out, recips_in = sem("recips_ready"), sem("recips_out"), sem("recips_in")
        attnT_ready, attnT_hi, attnT_lo = sem("attnT_ready"), sem("attnT_hi"), sem("attnT_lo")
        out_ready = sem("out_ready")
        stored = sem("stored")
        last_inverted, last_scaled = sem("last_inverted"), sem("last_scaled")
        last_hi, last_split = sem("last_hi"), sem("last_split")

        block = stack.enter_context(nc.Block())

        def steps(engine, step):
            step(batch(0), True, True, False)
            step(batch(1), True, True, True)
            with engine.Fori(1, B // 2 - 1) as i:
                step(Batch(2 * i, 0, i), True, True, True)
                step(Batch(2 * i + 1, 1, i), True, True, True)
            step(batch(B - 2), True, False, True)
            step(batch(B - 1), False, False, True)

        @block.sync
        def _(sp):
            def load_ctx(b, again):
                if again:
                    sp.wait_ge(nT_in_psum, DC * (b.n - 1))
                sp.dma_start(ctx_sb[:, b.parity, 0:SC - 1],
                             ctx[b.n, 0:(SC - 1) * P].rearrange("(c p) d -> p c d", p=P)
                             ).then_inc(ctx_in[b.parity], 16)
                sp.dma_start(ctx_sb[0:S_LAST, b.parity, SC - 1],
                             ctx[b.n, (SC - 1) * P:S]).then_inc(ctx_in[b.parity], 16)

            def load_xT(i, again):
                if again:
                    sp.wait_ge(xT_lo, DC * (i - 1))
                sp.dma_start(xT_raw[i % 2], xT[:, i * QCOLS:(i + 1) * QCOLS].rearrange(
                    "(k p) n -> p k n", p=P)).then_inc(xT_in[i % 2], 16)

            def weights(w):
                return w.rearrange("(k p) n -> p k n", p=P)

            for k in range(DC):
                sp.dma_start(wq_raw[:, k], wqT[k * P:(k + 1) * P]).then_inc(wq_in[k], 16)
                sp.dma_start(xT_raw[0][:, k], xT[k * P:(k + 1) * P, 0:QCOLS]).then_inc(xT_first[k], 16)
                if k == 0:
                    sp.dma_start(mask_u8[:], mask).then_inc(mask_in, 16)
            load_xT(1, False)
            sp.dma_start(gamma_sb[:], gamma).then_inc(small_in, 16)
            sp.dma_start(beta_sb[:], beta).then_inc(small_in, 16)
            sp.dma_start(gate_sb[:, 0:1], gate[None, :].to_broadcast([P, 1])).then_inc(small_in, 16)
            load_ctx(batch(0), False)
            for k in range(DC):
                sp.dma_start(wk_raw[k], wkT[k * P:(k + 1) * P]).then_inc(wk_in[k], 16)
            load_ctx(batch(1), False)
            sp.dma_start(wv_raw, weights(wvT)).then_inc(wv_in, 16)
            for i in range(2, QN):
                load_xT(i, True)
            sp.dma_start(wo_raw, weights(woT)).then_inc(wo_in, 16)
            def load_x(b, again):
                if again:
                    sp.wait_ge(stored, 16 * (b.n - 1))
                sp.dma_start(x_rows[0:T, b.parity], x[b.n]).then_inc(x_in[b.parity], 16)

            sp.wait_ge(wk_lo, DC)
            sp.wait_ge(kb_in_psum, 1)
            load_x(batch(0), False)
            load_x(batch(1), False)

            def sums_round_trip(b):
                sp.wait_ge(attn_kept, 2 * b.n + 2)
                flat = sums_dram[b.parity].rearrange("(a s g) t -> a s (g t)", a=2, s=2)
                for half in range(2):
                    row = 64 * half + HEAD_DIM
                    sp.dma_start(flat[half:half + 1], attn_raw[row:row + 1]).then_inc(sums_out, 16)
                sp.wait_ge(sums_out, 32 * b.n + 32)
                sp.dma_start(sums[:], sums_dram[b.parity]).then_inc(sums_in, 16)
                sp.wait_ge(recips_ready, b.n + 1)
                sp.dma_start(recip_dram[b.parity], recips[:]).then_inc(recips_out, 16)
                sp.wait_ge(recips_out, 16 * b.n + 16)
                back = recip_dram[b.parity].rearrange("(a s g) t -> a (s g t)", a=2, s=2)
                for half in range(2):
                    lo = 64 * half
                    sp.dma_start(recip_bc[lo:lo + HEAD_DIM].rearrange("p a n -> p (a n)"),
                                 back[half:half + 1].to_broadcast([HEAD_DIM, 2 * G * T])
                                 ).then_inc(recips_in, 16)

            def store(b):
                sp.wait_ge(out_ready, b.n + 1)
                sp.dma_start(out[b.n], x_rows[0:T, b.parity]).then_inc(stored, 16)

            def step(b, more, more2, prev):
                if more2:
                    load_ctx(b.after(2), True)
                if prev:
                    sums_round_trip(b.after(-1))
                    store(b.after(-1))
                    if more:
                        load_x(b.after(1), True)

            steps(sp, step)
            last = batch(B - 1)
            store(last)
            sp.wait_ge(stored, 16 * B)

        @block.tensor
        def _(pe):
            def split_product(dst, wh, wl, mh, ml, start, stop):
                nc.tensor.matmul(dst, wh, mh, start=start, stop=False)
                nc.tensor.matmul(dst, wh, ml, start=False, stop=False)
                return nc.tensor.matmul(dst, wl, mh, start=False, stop=stop)

            pe.wait_ge(ident_ready, 2)
            pe.wait_ge(mask_cast, 1)
            for c in range(SC):
                last = nc.tensor.transpose(mask_bank[:, c * B:(c + 1) * B], mask_f[:, c * P:(c + 1) * P],
                                           ident[0:B, 0:B])
            last.then_inc(maskT_in_psum, 1)

            def bank_free(b, u):
                if not (isinstance(b.n, int) and UNITS * b.n + u - 2 <= 0):
                    pe.wait_ge(drained, UNITS * b.n + u - 2)

            def transposes(b, first, last_chunk):
                pe.wait_ge(normed, b.n + 1)
                for k in range(first, last_chunk + 1):
                    u = U_NT + k
                    if not is_first(b):
                        bank_free(b, u)
                    for c in range(SC):
                        last = nc.tensor.transpose(nT_bank(b, k)[:, c * P:c * P + rows[c]],
                                                   ctx_sb[0:rows[c], b.parity, c, k * P:(k + 1) * P],
                                                   ident[0:rows[c], 0:rows[c]])
                    last.then_inc(nT_in_psum, 1)

            for i in range(QN):
                for k in range(DC):
                    if i == 0:
                        pe.wait_ge(wq_lo, k + 1)
                    pe.wait_ge(xT_lo, DC * i + k + 1)
                    for g in range(G):
                        if k == 0 and i == 1 and g == G - 1:
                            pe.wait_ge(mask_bias_ready, 1)
                        if k == 0 and i >= 2:
                            pe.wait_ge(q_kept, G * (i - 2) + g + 1)
                        last = split_product(q_banks[i % 2][g][:, 0:QCOLS],
                                             wqh[:, k, g * P:(g + 1) * P], wql[:, k, g * P:(g + 1) * P],
                                             nTh[:, k], nTl[:, k], k == 0, k == DC - 1)
                        if k == DC - 1 and g < G - 1:
                            last.then_inc(q_in_psum, 1)
                    last.then_inc(xT_used, 1)
                    if i == 0 and k == 0:
                        pe.wait_ge(maskT_kept, 1)
                        nc.tensor.matmul(mask_bank[:, SC * B:2 * SC * B], ones[:], maskT[:],
                                         start=True, stop=True).then_inc(count_in_psum, 1)
                    elif i == QN - 1 and k == DC - 2:
                        pe.wait_ge(q_kept, G * (QN - 1))
                        transposes(batch(0), 0, DC - 1)
            def k_projection(b, g):
                u = U_K + g
                if is_first(b) and g < 2:
                    pe.wait_ge(q_kept, G * (QN - 1) + g + 1)
                if g:
                    pe.wait_ge(drained, UNITS * b.n + max(DC, u - 2))
                for k in range(DC):
                    if g == 0:
                        pe.wait_ge(drained, UNITS * b.n + max(k + 1, u - 2))
                    last = split_product(ps_w[:, u % 3, 0:S_EVEN],
                                         wkh[:, k, g * P:(g + 1) * P], wkl[:, k, g * P:(g + 1) * P],
                                         nTh[:, k, 0:S_EVEN], nTl[:, k, 0:S_EVEN], k == 0, k == DC - 1)
                last.then_inc(k_in_psum, 1)

            def v_projection(b, c):
                u = U_V + c
                if c < SC - 1:
                    pe.wait_ge(drained, UNITS * b.n + U_K + 3 + c)
                elif not (isinstance(b.n, int) and b.n < 2):
                    pe.wait_ge(out_ready, b.n - 1)
                for k in range(DC):
                    at = slice(c * P, c * P + rows[c])
                    last = split_product(ps_w[0:rows[c], u % 3, :], nTh[:, k, at], nTl[:, k, at],
                                         wvh[:, k], wvl[:, k], k == 0, k == DC - 1)
                last.then_inc(v_in_psum, 1)

            def scores(b, g):
                if g == 0:
                    pe.wait_ge(drained, UNITS * b.n + U_K + G)
                    pe.wait_ge(qblk_ready, b.n + 1)
                for c in range(SC):
                    if not (is_first(b) and g == 0):
                        pe.wait_ge(s_kept, SC * (G * b.n + g - 1) + c + 1)
                    at = slice(c * P, (c + 1) * P)
                    split_product(ps_s[:, c, 0:GT], kTh[:, b.parity, g, at], kTl[:, b.parity, g, at],
                                  qblk_h[b.parity][:, g], qblk_l[b.parity][:, g], True, True
                                  ).then_inc(s_in_psum, 1)

            def weighted_values(b, g):
                pe.wait_ge(probs_ready, G * b.n + g + 1)
                if g == 0:
                    pe.wait_ge(drained, UNITS * b.n + UNITS)
                    if not is_first(b):
                        pe.wait_ge(attn_kept, 2 * b.n)
                for slot in range(2):
                    for c in range(SC):
                        for half in range(2):
                            j = 2 * slot + half
                            last = nc.tensor.matmul(
                                ps_av[64 * half:64 * half + OV, slot, g * T:(g + 1) * T],
                                v_sb[0:rows[c], b.parity, c, HG * g + j, 0:OV],
                                probs[0:rows[c], g, c, j * T:(j + 1) * T],
                                start=c == 0, stop=c == SC - 1)
                last.then_inc(av_done, 1)

            def last_weighted_values(b, g):
                pe.wait_ge(probs_ready, G * b.n + g + 1)
                if g == 0:
                    pe.wait_ge(drained, UNITS * b.n + UNITS)
                    pe.wait_ge(attn_kept, 2 * b.n)
                elif g == 2:
                    pe.wait_ge(s_kept, SC * (G * b.n + G))
                for c in range(SC):
                    for j in range(HG):
                        nc.tensor.matmul(last_banks[g][HEAD_DIM * j:HEAD_DIM * (j + 1), 0:T],
                                         v_sb[0:rows[c], b.parity, c, HG * g + j, 0:HEAD_DIM],
                                         probs[0:rows[c], g, c, j * T:(j + 1) * T],
                                         start=c == 0, stop=c == SC - 1)
                for c in range(SC):
                    for j in range(HG):
                        last = nc.tensor.matmul(last_banks[g][HEAD_DIM * j:HEAD_DIM * (j + 1), T:2 * T],
                                                ones[0:rows[c], 0:HEAD_DIM],
                                                probs[0:rows[c], g, c, j * T:(j + 1) * T],
                                                start=c == 0, stop=c == SC - 1)
                last.then_inc(av_done, 1)

            def out_projection(b):
                if is_last(b):
                    pe.wait_ge(s_kept, SC * G * B)
                    hi, lo = last_attnTh, last_attnTl
                else:
                    pe.wait_ge(attnT_lo, b.n + 1)
                    hi, lo = attnTh, attnTl
                for g in range(G):
                    if is_last(b):
                        pe.wait_ge(last_split, g + 1)
                    last = split_product(out_bank(b)[0:T], hi[:, g], lo[:, g],
                                         woh[:, g], wol[:, g], g == 0, g == G - 1)
                last.then_inc(out_in_psum, 1)

            pe.wait_ge(wk_lo, DC)
            for g0 in range(G):
                if g0 == 2:
                    for g in range(G):
                        for k in range(DC):
                            pe.wait_ge(wk_in[k], 16)
                            last = nc.tensor.matmul(ps_s[:, 1, g:g + 1], wk_raw[k][:, g * P:(g + 1) * P],
                                                    beta_sb[:, k:k + 1], start=k == 0, stop=k == DC - 1)
                    last.then_inc(kb_in_psum, 1)
                k_projection(batch(0), g0)
            pe.wait_ge(wv_in, 16)
            pe.wait_ge(beta_bc_ready, 1)
            for k in range(DC):
                last = nc.tensor.matmul(ps_s[:, 2, :], beta_bc[:, k], wv_raw[:, k], start=k == 0,
                                        stop=k == DC - 1)
            last.then_inc(vb_in_psum, 1)
            pe.wait_ge(wv_lo, DC)
            for c in range(SC):
                v_projection(batch(0), c)

            def step(b, more, more2, prev):
                n = b.after(1)
                if more:
                    transposes(n, 0, 1)
                scores(b, 0)
                if more:
                    transposes(n, 2, DC - 1)
                scores(b, 1)
                if more:
                    k_projection(n, 0)
                    k_projection(n, 1)
                scores(b, 2)
                if more:
                    k_projection(n, 2)
                    k_projection(n, 3)
                    weighted_values(b, 0)
                    scores(b, 3)
                    v_projection(n, 0)
                    weighted_values(b, 1)
                    v_projection(n, 1)
                    weighted_values(b, 2)
                    if prev:
                        pe.wait_ge(drained, UNITS * n.n + U_K + 2)
                        out_projection(b.after(-1))
                    weighted_values(b, 3)
                    if more2:
                        v_projection(n, 2)
                else:
                    v_projection(b, 2)
                    scores(b, 3)
                    for g in range(G):
                        last_weighted_values(b, g)
                    pe.wait_ge(drained, UNITS * b.n + 2 * DC + 1)
                    out_projection(b.after(-1))
                    out_projection(b)

            pe.wait_ge(vb_ready, 1)
            pe.wait_ge(kb_ready, 1)
            pe.wait_ge(wo_lo, DC)
            steps(pe, step)

        @block.scalar
        def _(act):
            def split_xT(i):
                for k in range(DC):
                    if i == 0:
                        act.wait_ge(wq_in[k], 16)
                        nc.scalar.copy(wqh[:, k], wq_raw[:, k]).then_inc(wq_hi, 1)
                        act.wait_ge(xT_first[k], 16)
                    elif k == 0:
                        act.wait_ge(xT_in[i % 2], 16 * ((i + 1) // 2))
                    if i >= 1:
                        act.wait_ge(xT_used, DC * (i - 1) + k + 1)
                    nc.scalar.copy(nTh[:, k], xT_raw[i % 2][:, k]).then_inc(xT_hi, 1)
                    if i == 2:
                        act.wait_ge(wk_in[k], 16)
                        nc.scalar.activation(wkh[:, k], wk_raw[k], ACT.Identity,
                                             scale=gamma_sb[:, k:k + 1]).then_inc(wk_hi, 1)
                    elif i == 3:
                        act.wait_ge(wv_in, 16)
                        nc.scalar.activation(wvh[:, k], wv_raw[:, k], ACT.Identity,
                                             scale=gamma_sb[:, k:k + 1]).then_inc(wv_hi, 1)

            def keep_q(i):
                for g in range(G):
                    if g < G - 1:
                        act.wait_ge(q_in_psum, (G - 1) * i + g + 1)
                    else:
                        act.wait_ge(xT_used, DC * (i + 1))
                    nc.scalar.copy(q_sb[:, g, i * QCOLS:(i + 1) * QCOLS],
                                   q_banks[i % 2][g][:, 0:QCOLS]).then_inc(q_kept, 1)

            split_xT(0)
            act.wait_ge(small_in, 48)
            nc.scalar.activation(gate_sb[:, 1:2], gate_sb[:, 0:1], ACT.Tanh).then_inc(gate_ready, 1)
            split_xT(1)
            keep_q(0)
            split_xT(2)
            keep_q(1)
            split_xT(3)
            keep_q(2)
            act.wait_ge(wo_in, 16)
            for k in range(DC):
                nc.scalar.copy(woh[:, k], wo_raw[:, k]).then_inc(wo_hi, 1)

            def keep_nT_hi(b, first, last_chunk):
                for k in range(first, last_chunk + 1):
                    act.wait_ge(nT_in_psum, DC * b.n + k + 1)
                    if is_first(b):
                        act.wait_ge(xT_used, DC * (QN - 1) + k + 1)
                    nc.scalar.copy(nTh[:, k, 0:S], nT_bank(b, k)[:, 0:S]).then_inc(nT_hi, 1)

            def keep_k_hi(b, g):
                act.wait_ge(k_in_psum, G * b.n + g + 1)
                nc.scalar.activation(kTh[:, b.parity, g, 0:S], ps_w[:, (U_K + g) % 3, 0:S],
                                     ACT.Identity, bias=k_bias[:, g:g + 1]).then_inc(k_hi, 1)

            def block_q_hi(b):
                for j in range(HG):
                    at = slice(HEAD_DIM * j, HEAD_DIM * (j + 1))
                    nc.scalar.copy(qblk_h[b.parity][at, :, j], q_sb[at, :, bass.ds(b.n * T, T)]
                                   ).then_inc(qblk_hi, 1)
                nc.scalar.copy(mask_now[:, b.parity], mask_bias[:, bass.ds(b.n * SC, SC)]
                               ).then_inc(mask_copied, 1)

            def keep_scores(b, g):
                if not is_first(b):
                    act.wait_ge(av_done, G * (b.n - 1) + g + 1)
                if g == 0:
                    act.wait_ge(mask_copied, b.n + 1)
                for c in range(SC):
                    act.wait_ge(s_in_psum, SC * (G * b.n + g) + c + 1)
                    nc.scalar.activation(probs[:, g, c], ps_s[:, c, 0:GT], ACT.Identity,
                                         bias=mask_now[:, b.parity, c:c + 1]).then_inc(s_kept, 1)

            def exponentials(b, g):
                act.wait_ge(shifted, G * b.n + g + 1)
                nc.scalar.activation(probs[:, g], probs[:, g], ACT.Exp,
                                     scale=scale).then_inc(probs_ready, 1)

            def split_attn_hi(b):
                act.wait_ge(attnT_ready, b.n + 1)
                nc.scalar.copy(attnTh[:], attnT[:]).then_inc(attnT_hi, 1)

            def keep_attn(b):
                act.wait_ge(av_done, G * b.n + G)
                if not is_first(b):
                    act.wait_ge(attnT_ready, b.n)
                for half in range(2):
                    at = slice(64 * half, 64 * half + OV)
                    nc.scalar.copy(attn_raw[at], ps_av[at, :, 0:G * T]).then_inc(attn_kept, 1)

            keep_nT_hi(batch(0), 0, DC - 1)
            keep_q(3)
            act.wait_ge(mask_bias_ready, 1)
            act.wait_ge(pads_ready, 1)
            act.wait_ge(qblk_zeroed, 1)
            block_q_hi(batch(0))
            act.wait_ge(kb_ready, 1)
            for g in range(G):
                keep_k_hi(batch(0), g)
            act.wait_ge(qblk_zeroed, 2)

            def step(b, more, more2, prev):
                n = b.after(1)
                if more:
                    keep_nT_hi(n, 0, 1)
                keep_scores(b, 0)
                if not more:
                    keep_attn(b.after(-1))
                if more:
                    keep_nT_hi(n, 2, DC - 1)
                keep_scores(b, 1)
                if more:
                    keep_k_hi(n, 0)
                    keep_k_hi(n, 1)
                keep_scores(b, 2)
                exponentials(b, 0)
                if more:
                    keep_k_hi(n, 2)
                    keep_k_hi(n, 3)
                keep_scores(b, 3)
                exponentials(b, 1)
                if prev and more:
                    split_attn_hi(b.after(-1))
                if more:
                    block_q_hi(n)
                exponentials(b, 2)
                exponentials(b, 3)
                if not more:
                    split_attn_hi(b.after(-1))
                if more2:
                    keep_attn(b)

            steps(act, step)
            for g in range(G):
                act.wait_ge(last_scaled, g + 1)
                nc.scalar.copy(last_attnTh[:, g], attnT[:, g]).then_inc(last_hi, 1)

        @block.gpsimd
        def _(pool):
            nc.gpsimd.memset(ident[:], 0.0).then_inc(ident_ready, 1)
            pool.wait_ge(ident_ready, 1)
            nc.gpsimd.affine_select(out=ident[:], in_=ident[:], compare_op=ALU.not_equal, fill=1.0,
                                    base=0, pattern=[[-1, P]], channel_multiplier=1
                                    ).then_inc(ident_ready, 1)
            nc.gpsimd.memset(qblk_even[:].bitcast(F32), 0.0).then_inc(qblk_zeroed, 1)
            pool.wait_ge(xT_used, DC * QN)
            nc.gpsimd.memset(wqh[:].bitcast(F32), 0.0)
            nc.gpsimd.memset(wql[:].bitcast(F32), 0.0).then_inc(qblk_zeroed, 1)

            def row_maximum(b, g):
                if not (is_first(b) and g < 2):
                    pool.wait_ge(shifted, G * b.n + g - 1)
                pool.wait_ge(colmax_ready, G * b.n + g + 1)
                pool.sem_inc(waited_pool, 1)
                nc.gpsimd.partition_all_reduce(rowmax[:, g % 2], colmax[:, g % 2], P,
                                               bass.bass_isa.ReduceOp.max).then_inc(rowmax_ready, 1)
                pool.wait_ge(rowmax_ready, G * b.n + g + 1)

            def step(b, more, more2, prev):
                for g in range(G):
                    row_maximum(b, g)

            steps(pool, step)

        @block.vector
        def _(dve):
            def layer_norm_stats(b, c):
                if c == 0:
                    dve.wait_ge(ctx_in[b.parity], 32 * (b.pair + 1))
                op = nc.vector.bn_stats(stats[0:rows[c], c], ctx_sb[0:rows[c], b.parity, c])
                if c == SC - 1:
                    op.then_inc(ln_step, 1)

            def layer_norm_step(b, i):
                dve.wait_ge(ln_step, LN_STEPS * b.n + i + 1)
                if i == 0:
                    dve.sem_inc(waited_dve, 1)
                    for c in range(SC):
                        op = nc.vector.bn_aggr(mean_var[0:rows[c], c], stats[0:rows[c], c])
                elif i == 1:
                    op = nc.vector.tensor_scalar(var_eps[:], mean_var[:, :, 1], LN_EPS, None, ALU.add)
                elif i == 2:
                    op = nc.vector.tensor_scalar(half_bits[:], var_eps[:].bitcast(I32), 1, None,
                                                 ALU.logical_shift_right)
                elif i == 3:
                    op = nc.vector.tensor_scalar(rstd[:].bitcast(I32), half_bits[:], -1.0, RSQRT_MAGIC,
                                                 ALU.mult, ALU.add)
                elif i % 3 == 1:
                    op = nc.vector.scalar_tensor_tensor(newton_a[:], rstd[:], -0.5, rstd[:], ALU.mult,
                                                        ALU.mult)
                elif i % 3 == 2:
                    op = nc.vector.tensor_tensor(newton_b[:], newton_a[:], var_eps[:], ALU.mult)
                else:
                    op = nc.vector.scalar_tensor_tensor(rstd[:], newton_b[:], 1.5, rstd[:], ALU.add,
                                                        ALU.mult)
                op.then_inc(ln_step, 1)

            def layer_norm_apply(b):
                dve.wait_ge(ln_step, LN_STEPS * b.n + LN_STEPS)
                for c in range(SC):
                    at = ctx_sb[0:rows[c], b.parity, c]
                    last = nc.vector.tensor_scalar(at, at, mean_var[0:rows[c], c, 0:1],
                                                   rstd[0:rows[c], c:c + 1], ALU.subtract, ALU.mult)
                last.then_inc(normed, 1)

            def layer_norm(b):
                for c in range(SC):
                    layer_norm_stats(b, c)
                for i in range(RSTD_STEPS):
                    layer_norm_step(b, i)
                layer_norm_apply(b)

            nc.vector.memset(ones[:], 1.0)
            nc.vector.memset(mean_var[:], 1.0).then_inc(setup, 1)
            nc.vector.memset(mask_f, 0.0).then_inc(setup, 1)
            dve.wait_ge(mask_in, 16)
            dve.wait_ge(setup, 2)
            nc.vector.tensor_copy(mask_f[:, 0:S], mask_u8[:]).then_inc(mask_cast, 1)

            def split_xT(i):
                for k in range(DC):
                    if i == 0:
                        dve.wait_ge(wq_hi, k + 1)
                        nc.vector.tensor_tensor(wql[:, k], wq_raw[:, k], wqh[:, k],
                                                ALU.subtract).then_inc(wq_lo, 1)
                    dve.wait_ge(xT_hi, DC * i + k + 1)
                    nc.vector.tensor_tensor(nTl[:, k], xT_raw[i % 2][:, k], nTh[:, k],
                                            ALU.subtract).then_inc(xT_lo, 1)
                    if i == 0 and k == 0:
                        dve.wait_ge(maskT_in_psum, 1)
                        nc.vector.tensor_copy(maskT[:], mask_bank[:, 0:SC * B]).then_inc(maskT_kept, 1)
                    if i == 2:
                        dve.wait_ge(wk_hi, k + 1)
                        nc.vector.scalar_tensor_tensor(wkl[:, k], wk_raw[k], gamma_sb[:, k:k + 1],
                                                       wkh[:, k], ALU.mult, ALU.subtract
                                                       ).then_inc(wk_lo, 1)
                    elif i == 3:
                        dve.wait_ge(wv_hi, k + 1)
                        nc.vector.scalar_tensor_tensor(wvl[:, k], wv_raw[:, k], gamma_sb[:, k:k + 1],
                                                       wvh[:, k], ALU.mult, ALU.subtract
                                                       ).then_inc(wv_lo, 1)

            split_xT(0)
            by_batch = maskT[:].rearrange("p (c b) -> p b c", c=SC)
            biases = mask_bias[:].rearrange("p (b c) -> p b c", c=SC)
            dve.wait_ge(maskT_kept, 1)
            nc.vector.tensor_scalar(biases, by_batch, 1.0, -MASKED, ALU.subtract, ALU.mult
                                    ).then_inc(setup, 1)
            dve.wait_ge(count_in_psum, 1)
            nc.vector.tensor_reduce(key_count[:], mask_bank[:, SC * B:2 * SC * B].rearrange(
                "p (c b) -> p b c", c=SC), mybir.AxisListType.X, ALU.add).then_inc(setup, 1)
            dve.wait_ge(setup, 4)
            nc.vector.reciprocal(key_count[:], key_count[:]).then_inc(setup, 1)
            dve.wait_ge(setup, 5)
            nc.vector.scalar_tensor_tensor(biases, key_count[:].unsqueeze(2).to_broadcast([P, B, SC]),
                                           0.0, biases, ALU.mult, ALU.add).then_inc(mask_bias_ready, 1)
            dve.wait_ge(ident_ready, 2)
            dve.wait_ge(small_in, 48)
            for k in range(DC):
                last = nc.vector.tensor_scalar(beta_bc[:, k], ident[:], 0.0, beta_sb[:, k:k + 1],
                                               ALU.mult, ALU.add)
            last.then_inc(beta_bc_ready, 1)
            split_xT(1)
            layer_norm(batch(0))
            split_xT(2)
            split_xT(3)
            dve.wait_ge(wk_lo, DC)
            nc.vector.memset(kTh[:, :, :, S:SC * P].bitcast(F32), 0.0)
            nc.vector.memset(kTl[:, :, :, S:SC * P].bitcast(F32), 0.0).then_inc(pads_ready, 1)
            dve.wait_ge(xT_lo, DC * QN)
            nc.vector.memset(v_sb[:, :, :, :, HEAD_DIM:HEAD_DIM + 1], 1.0).then_inc(setup, 1)
            for k in range(DC):
                dve.wait_ge(wo_hi, k + 1)
                nc.vector.tensor_tensor(wol[:, k], wo_raw[:, k], woh[:, k], ALU.subtract).then_inc(wo_lo, 1)
            def block_q_lo(b, j):
                at = slice(HEAD_DIM * j, HEAD_DIM * (j + 1))
                dve.wait_ge(qblk_hi, HG * b.n + j + 1)
                op = nc.vector.tensor_tensor(qblk_l[b.parity][at, :, j],
                                             q_sb[at, :, bass.ds(b.n * T, T)],
                                             qblk_h[b.parity][at, :, j], ALU.subtract)
                if j == HG - 1:
                    op.then_inc(qblk_ready, 1)

            def keep_nT_lo(b, first, last_chunk):
                for k in range(first, last_chunk + 1):
                    dve.wait_ge(nT_hi, DC * b.n + k + 1)
                    nc.vector.tensor_tensor(nTl[:, k, 0:S], nT_bank(b, k)[:, 0:S],
                                            nTh[:, k, 0:S], ALU.subtract).then_inc(drained, 1)

            def keep_k_lo(b, g):
                dve.wait_ge(k_hi, G * b.n + g + 1)
                nc.vector.scalar_tensor_tensor(kTl[:, b.parity, g, 0:S], ps_w[:, (U_K + g) % 3, 0:S],
                                               k_bias[:, g:g + 1], kTh[:, b.parity, g, 0:S],
                                               ALU.add, ALU.subtract).then_inc(drained, 1)

            def keep_v(b, c):
                dve.wait_ge(v_in_psum, SC * b.n + c + 1)
                nc.vector.tensor_tensor(
                    v_sb[0:rows[c], b.parity, c, :, 0:HEAD_DIM],
                    ps_w[0:rows[c], (U_V + c) % 3, :].rearrange("p (h d) -> p h d", h=H),
                    v_bias[0:rows[c]].rearrange("p (h d) -> p h d", h=H), ALU.add).then_inc(drained, 1)

            def column_maximum(b, g):
                dve.wait_ge(s_kept, SC * (G * b.n + g) + 2)
                nc.vector.tensor_tensor(colmax[:, g % 2], probs[:, g, 0], probs[:, g, 1],
                                        ALU.max).then_inc(max_partial, 1)
                dve.wait_ge(s_kept, SC * (G * b.n + g) + 3)
                dve.wait_ge(max_partial, G * b.n + g + 1)
                nc.vector.tensor_tensor(colmax[:, g % 2], colmax[:, g % 2], probs[:, g, 2],
                                        ALU.max).then_inc(colmax_ready, 1)

            def shift(b, g):
                dve.wait_ge(rowmax_ready, G * b.n + g + 1)
                nc.vector.tensor_tensor(probs[:, g], probs[:, g],
                                        rowmax[:, g % 2:g % 2 + 1].to_broadcast([P, SC, GT]),
                                        ALU.subtract).then_inc(shifted, 1)

            def invert_sums(b):
                dve.wait_ge(sums_in, 16 * b.n + 16)
                nc.vector.reciprocal(recips[:], sums[:]).then_inc(recips_ready, 1)

            def scale_attn(b):
                dve.wait_ge(recips_in, 32 * b.n + 32)
                if not is_first(b):
                    dve.wait_ge(out_in_psum, b.n)
                for slot in range(2):
                    for half in range(2):
                        j = 2 * slot + half
                        at = slice(64 * half, 64 * half + HEAD_DIM)
                        last = nc.vector.tensor_tensor(
                            attnT[HEAD_DIM * j:HEAD_DIM * (j + 1)].rearrange("p g t -> p (g t)"),
                            attn_raw[at, slot], recip_bc[at, slot], ALU.mult)
                last.then_inc(attnT_ready, 1)

            def split_attn_lo(b):
                dve.wait_ge(attnT_hi, b.n + 1)
                nc.vector.tensor_tensor(attnTl[:], attnT[:], attnTh[:], ALU.subtract
                                        ).then_inc(attnT_lo, 1)

            def gated_residual(b):
                dve.wait_ge(out_in_psum, b.n + 1)
                dve.wait_ge(x_in[b.parity], 16 * (b.pair + 1))
                nc.vector.scalar_tensor_tensor(x_rows[0:T, b.parity], out_bank(b)[0:T],
                                               gate_sb[0:T, 1:2], x_rows[0:T, b.parity],
                                               ALU.mult, ALU.add).then_inc(out_ready, 1)

            dve.wait_ge(gate_ready, 1)
            first, second = batch(0), batch(1)
            keep_nT_lo(first, 0, DC - 1)
            for j in range(HG):
                block_q_lo(first, j)
            dve.wait_ge(kb_in_psum, 1)
            nc.vector.tensor_copy(k_bias[:], ps_s[:, 1, 0:G]).then_inc(kb_ready, 1)
            dve.wait_ge(kb_ready, 1)
            keep_k_lo(first, 0)
            keep_k_lo(first, 1)
            for c in range(SC):
                layer_norm_stats(second, c)
            keep_k_lo(first, 2)
            keep_k_lo(first, 3)
            for i in range(RSTD_STEPS):
                layer_norm_step(second, i)
            dve.wait_ge(vb_in_psum, 1)
            nc.vector.tensor_copy(v_bias[:], ps_s[:, 2, :]).then_inc(vb_ready, 1)
            dve.wait_ge(vb_ready, 1)
            dve.wait_ge(setup, 6)
            keep_v(first, 0)
            layer_norm_apply(second)
            keep_v(first, 1)
            keep_v(first, 2)

            def last_invert(g):
                dve.wait_ge(av_done, G * (B - 1) + g + 1)
                nc.vector.reciprocal(last_recip[:, g * T:(g + 1) * T], last_banks[g][:, T:2 * T]
                                     ).then_inc(last_inverted, 1)

            def last_scale(g):
                dve.wait_ge(last_inverted, g + 1)
                if g == 0:
                    dve.wait_ge(attnT_lo, B - 1)
                nc.vector.tensor_tensor(attnT[:, g], last_banks[g][:, 0:T],
                                        last_recip[:, g * T:(g + 1) * T], ALU.mult
                                        ).then_inc(last_scaled, 1)

            def last_split_lo(g):
                dve.wait_ge(last_hi, g + 1)
                nc.vector.tensor_tensor(last_attnTl[:, g], attnT[:, g], last_attnTh[:, g], ALU.subtract
                                        ).then_inc(last_split, 1)

            def step(b, more, more2, prev):
                n = b.after(1)

                def ln(*which):
                    if more2:
                        for i in which:
                            layer_norm_step(b.after(2), i)

                def ln_stats(c):
                    if more2:
                        layer_norm_stats(b.after(2), c)

                keep_nT_lo(n, 0, DC - 1)
                column_maximum(b, 0)
                column_maximum(b, 1)
                if prev:
                    invert_sums(b.after(-1))
                keep_k_lo(n, 0)
                ln_stats(0)
                keep_k_lo(n, 1)
                shift(b, 0)
                column_maximum(b, 2)
                ln_stats(1)
                shift(b, 1)
                keep_k_lo(n, 2)
                if prev:
                    scale_attn(b.after(-1))
                ln_stats(2)
                keep_k_lo(n, 3)
                column_maximum(b, 3)
                if prev:
                    split_attn_lo(b.after(-1))
                ln(0)
                shift(b, 2)
                ln(1)
                keep_v(n, 0)
                ln(2)
                block_q_lo(n, 0)
                ln(3)
                block_q_lo(n, 1)
                ln(4)
                block_q_lo(n, 2)
                ln(5)
                block_q_lo(n, 3)
                ln(6)
                shift(b, 3)
                ln(7)
                keep_v(n, 1)
                ln(8)
                if prev:
                    gated_residual(b.after(-1))
                ln(*range(9, RSTD_STEPS))
                if more2:
                    layer_norm_apply(b.after(2))
                    keep_v(n, 2)

            def last_step(b):
                column_maximum(b, 0)
                column_maximum(b, 1)
                shift(b, 0)
                column_maximum(b, 2)
                invert_sums(b.after(-1))
                shift(b, 1)
                column_maximum(b, 3)
                keep_v(b, 2)
                shift(b, 2)
                shift(b, 3)
                scale_attn(b.after(-1))
                last_invert(0)
                split_attn_lo(b.after(-1))
                last_scale(0)
                last_invert(1)
                last_scale(1)
                last_split_lo(0)
                last_invert(2)
                last_scale(2)
                last_split_lo(1)
                last_invert(3)
                last_scale(3)
                last_split_lo(2)
                last_split_lo(3)
                gated_residual(b.after(-1))
                gated_residual(b)

            steps(dve, lambda b, more, more2, prev: step(b, more, more2, prev) if more else last_step(b))


_INS = ["x", "xT", "ctx", "mask", "wqT", "wkT", "wvT", "woT", "gamma", "beta", "gate"]


def kernel(**inputs):
    import numpy as np
    import concourse.bacc as bacc
    from concourse.bass_utils import run_bass_kernel_spmd

    x = np.asarray(inputs["x"])
    B, T, D = x.shape
    laid = {
        "x": x,
        "xT": x.transpose(2, 0, 1).reshape(D, B * T),
        "ctx": np.asarray(inputs["ctx_2048"]),
        "mask": np.asarray(inputs["mask_BxS2_bf1"]).view(np.uint8),
        "wqT": np.asarray(inputs["L0_xattn_Wq"]).T,
        "wkT": np.asarray(inputs["L0_xattn_Wk"]).T,
        "wvT": np.asarray(inputs["L0_xattn_Wv"]).T,
        "woT": np.asarray(inputs["L0_xattn_Wo"]).T,
        "gamma": np.asarray(inputs["L0_xattn_ln_gamma"]).reshape(D // P, P).T,
        "beta": np.asarray(inputs["L0_xattn_ln_beta"]).reshape(D // P, P).T,
        "gate": np.asarray(inputs["L0_xattn_gate"]),
    }
    nc = bacc.Bacc("TRN2", target_bir_lowering=False, num_devices=1)
    arrays, args = {}, []
    for name in _INS:
        a = np.ascontiguousarray(laid[name])
        arrays["in_" + name] = a
        args.append(nc.dram_tensor("in_" + name, a.shape, mybir.dt.from_np(a.dtype),
                                   kind="ExternalInput").ap())
    args.append(nc.dram_tensor("out_rows_dram", (B, T, D), F32, kind="ExternalOutput").ap())
    xattn_program(nc, *args)
    r = run_bass_kernel_spmd(nc, [arrays], core_ids=[0])
    return r.results[0]["out_rows_dram"]
```
